# Optimizing a Trainium2 kernel written in Bass

```python
import numpy as np
import jax
import jax.numpy as jnp

def _softmax(x, axis=-1):
    return jax.nn.softmax(x, axis=axis)

def _gelu(x):
    return jax.nn.gelu(x, approximate=True)

def _silu(x):
    return jax.nn.silu(x)

def _sigmoid(x):
    return jax.nn.sigmoid(x)

def _layernorm(x, axis=-1, eps=1e-05):
    m = jnp.mean(x, axis=axis, keepdims=True)
    v = jnp.var(x, axis=axis, keepdims=True)
    return (x - m) / jnp.sqrt(v + eps)

def _scatter_add(tgt, idx, src, axis=0):
    return tgt.at[idx].add(src)

def _segment_sum(src, seg, n):
    return jax.ops.segment_sum(src, seg, n)
kernel_name = 'mk_xattn_ffn_d1_seqx_r4_f7578e'

def setup_inputs(seed: int=0):
    np.random.seed(seed)
    _w = jnp.asarray

    def _rec_inputs():
        import jax
        import jax.numpy as jnp
        _rk = jax.random.key(seed)
        x = 7.22e-05 + 1 * jax.random.normal(jax.random.fold_in(_rk, 1), (4, 512, 512), jnp.float32)
        _lenS = 512 - jax.random.randint(jax.random.fold_in(_rk, 7), (4,), 0, max(1, 512 // 4) + 1, jnp.int32)
        _lenS2 = 512 - jax.random.randint(jax.random.fold_in(_rk, 8), (4,), 0, max(1, 512 // 4) + 1, jnp.int32)
        _ctx_2048P = jax.random.normal(jax.random.fold_in(_rk, 11), (4, 16, 512), jnp.float32)
        _ctx_2048c = jax.random.dirichlet(jax.random.fold_in(_rk, 511), 0.3 * jnp.ones((16,), jnp.float32), (4, 512))
        _ctx_2048t = jnp.einsum('bsk,bkd->bsd', _ctx_2048c, _ctx_2048P)
        _ctx_2048t = _ctx_2048t * jax.lax.rsqrt(jnp.mean(jnp.square(_ctx_2048t)) + 1e-12) * 0.953939
        ctx_2048 = 4.13588e-05 + 0.999923 * (_ctx_2048t + 0.3 * jax.random.normal(jax.random.fold_in(_rk, 611), (4, 512, 512), jnp.float32))
        return (x, ctx_2048)
    x, ctx_2048 = _rec_inputs()

    def _L0_xattn_setup():
        import jax, jax.numpy as jnp
        import numpy as np
        N_HEAD = 8
        ALPHA = 5.0
        EPS = 1e-12

        def _l2norm(x, axis):
            n = jnp.sqrt(jnp.sum(x * x, axis=axis, keepdims=True))
            return x / jnp.maximum(n, EPS)
        key = jax.random.key(seed)
        kq, kk, kv = jax.random.split(key, 3)
        B, D, T = (4, 256, 512)
        q = jax.random.normal(kq, (B, D, T), dtype=jnp.float32)
        k = jax.random.normal(kk, (B, D, T), dtype=jnp.float32)
        v = jax.random.normal(kv, (B, D, T), dtype=jnp.float32)
        return {'q': q, 'k': k, 'v': v}
    _L0_xattn_all = _L0_xattn_setup()
    _L0_xattn_in = {k: v for k, v in _L0_xattn_all.items() if k in ()}
    del _L0_xattn_all

    def _L0_ffn_setup():
        import jax, jax.numpy as jnp
        import numpy as np
        B, T, D, E, H = (4, 512, 512, 4, 2048)
        TOPK = 2
        CAPACITY_FACTOR = 1
        key = jax.random.key(seed)
        k0, k1, k2, k3 = jax.random.split(key, 4)
        x = jax.random.normal(k0, (B, T, D), dtype=jnp.float32)
        Wg = jax.random.normal(k1, (D, E), dtype=jnp.float32) * 0.02
        bg = jnp.zeros((E,), dtype=jnp.float32)
        W1 = jax.random.normal(k2, (E, D, H), dtype=jnp.float32) * (1.0 / np.sqrt(D))
        W2 = jax.random.normal(k3, (E, H, D), dtype=jnp.float32) * (1.0 / np.sqrt(H))
        return {'x': x, 'Wg': Wg, 'bg': bg, 'W1': W1, 'W2': W2}
    _L0_ffn_all = _L0_ffn_setup()
    _L0_ffn_in = {k: v for k, v in _L0_ffn_all.items() if k in ('Wg', 'bg', 'W1', 'W2')}
    del _L0_ffn_all
    return {'x': x, 'ctx_2048': ctx_2048, 'L0_ffn_Wg': _L0_ffn_in['Wg'], 'L0_ffn_bg': _L0_ffn_in['bg'], 'L0_ffn_W1': _L0_ffn_in['W1'], 'L0_ffn_W2': _L0_ffn_in['W2']}

def reference(x, ctx_2048, L0_ffn_Wg, L0_ffn_bg, L0_ffn_W1, L0_ffn_W2):
    import jax
    import jax.numpy as jnp

    def _L0_xattn_ref(q, k, v):
        import jax, jax.numpy as jnp
        import numpy as np
        N_HEAD = 8
        ALPHA = 5.0
        EPS = 1e-12

        def _l2norm(x, axis):
            n = jnp.sqrt(jnp.sum(x * x, axis=axis, keepdims=True))
            return x / jnp.maximum(n, EPS)
        B, D, Tq = q.shape
        Tk = k.shape[-1]
        Dv = v.shape[-2]
        h = N_HEAD
        d = D // h
        dv = Dv // h
        qh = q.reshape(B, h, d, Tq)
        kh = k.reshape(B, h, d, Tk)
        vh = v.reshape(B, h, dv, Tk)
        qn = _l2norm(qh, axis=-2)
        kn = _l2norm(kh, axis=-2)
        qk = ALPHA * jnp.einsum('bhdq,bhdk->bhqk', qn, kn)
        sm = jax.nn.softmax(qk, axis=-1)
        out = jnp.einsum('bhqk,bhdk->bhdq', sm, vh)
        return out.reshape(B, Dv, Tq)

    def _L0_ffn_ref(x, Wg, bg, W1, W2):
        import jax, jax.numpy as jnp
        import numpy as np
        B, T, D, E, H = (4, 512, 512, 4, 2048)
        TOPK = 2
        CAPACITY_FACTOR = 1
        Bq, Tq, Dq = x.shape
        N = Bq * Tq
        capacity = int(N * CAPACITY_FACTOR / E)
        flat_x = x.reshape(N, Dq)
        logits = flat_x @ Wg + bg
        top_vals, top_idx = jax.lax.top_k(logits, TOPK)
        sparse = jnp.full_like(logits, -jnp.inf)
        sparse = sparse.at[jnp.arange(N)[:, None], top_idx].set(top_vals)
        probs = jax.nn.softmax(sparse, axis=-1)
        out = jnp.zeros_like(flat_x)
        for i in range(E):
            assigned = (top_idx == i).any(axis=-1)
            score = jnp.where(assigned, probs[:, i], -jnp.inf)
            sel_p, sel_idx = jax.lax.top_k(score, capacity)
            p = jnp.where(jnp.isfinite(sel_p), sel_p, 0.0)[:, None]
            tok = flat_x[sel_idx]
            h = jax.nn.gelu(tok @ W1[i], approximate=False)
            y = h @ W2[i] * p
            out = out.at[sel_idx].add(y)
        return out.reshape(Bq, Tq, Dq)
    x = x + _L0_xattn_ref(_layernorm(x, axis=-1), ctx_2048, ctx_2048)
    x = x + _L0_ffn_ref(_layernorm(x, axis=-1), L0_ffn_Wg, L0_ffn_bg, L0_ffn_W1, L0_ffn_W2)
    return x

_drawn_inputs = setup_inputs


def setup_inputs(seed=0):
    import zlib

    import numpy as np

    out = dict(_drawn_inputs(seed))
    spreads = {'L0_ffn_bg': (0.0, 0.1)}
    factors = {}
    for name, (base, spread) in spreads.items():
        noise = np.random.default_rng([zlib.crc32(name.encode()), seed]).standard_normal(out[name].shape)
        drawn = base * np.exp(spread * noise) if base else spread * noise
        out[name] = jnp.asarray(drawn.astype(out[name].dtype))
    for name, factor in factors.items():
        out[name] = (out[name] * factor).astype(out[name].dtype)
    return out
```

```python
from contextlib import ExitStack

import concourse.bass as bass
from concourse import mybir

F32 = mybir.dt.float32
F32R = mybir.dt.float32r
I32 = mybir.dt.int32
U32 = mybir.dt.uint32
ALU = mybir.AluOpType
ACT = mybir.ActivationFunctionType
AX_X = mybir.AxisListType.X

P = 128
B, S, D = 4, 512, 512
HEADS = 8
DH = S // HEADS
ALPHA = 5.0
NORM_EPS2 = 1e-24
LN_EPS = 1e-5
N_TOK = B * S
UNITS = N_TOK // P
TT = D // P
E, H = 4, 2048
CAP = N_TOK // E
ST = CAP // P
KD = D // P
MT = H // P
CHUNK_M = 2
CHUNKS = MT // CHUNK_M
RAW_BUFS, SPLIT_BUFS = 2, 4
AHEAD = 2
XT_AT = 8
CW = CHUNK_M * P
HALF = KD * CW

KEY_LO, KEY_RANGE, WAYS, ROUNDS = -17.0, 34.0, 32, 6
KEY_CLAMP = 16.64
KEY_OUT = -64.0
NO_SLOT = 4096.0

NARROW = 64
REP = NARROW // 2

C_IDENT, C_TRI, C_ONES, C_BLOCK, C_IOTA = (P * n for n in range(5))
C_HEAD = 5 * P
C_ROWS = C_HEAD + NARROW
C_KVEC = C_ROWS + 2 * NARROW
C_PICK = C_KVEC + 2
C_TOK = C_PICK + E
C_TIE = C_TOK + UNITS
C_OFFD = C_TIE + E * E
C_RESET = C_OFFD + E * E
C_ALL = C_RESET + E * 2 * UNITS


def constants():
    import numpy as np

    c = np.zeros((P, C_ALL), np.float32)
    p = np.arange(P)
    c[:, C_IDENT:C_IDENT + P] = np.eye(P)
    c[:, C_TRI:C_TRI + P] = p[:, None] < p[None, :]
    c[:, C_ONES:C_ONES + P] = 1
    c[:, C_BLOCK:C_BLOCK + P] = p[:, None] // WAYS == p[None, :] // WAYS
    c[:, C_IOTA:C_IOTA + P] = p[None, :]
    c[:, C_HEAD:C_HEAD + NARROW] = p[:, None] // DH == np.arange(NARROW)[None, :] // REP
    c[DH, C_ROWS:C_ROWS + NARROW] = 1
    c[0, C_ROWS + NARROW:C_ROWS + 2 * NARROW] = 1
    c[:, C_KVEC] = p % WAYS + 1
    c[:, C_PICK:C_PICK + E] = p[:, None] == WAYS * np.arange(E)[None, :]
    c[:, C_TOK:C_TOK + UNITS] = p[:, None] + P * np.arange(UNITS)[None, :] + 1
    i, j = np.divmod(np.arange(E * E), E)
    c[:, C_TIE:C_TIE + E * E] = j < i
    c[:, C_OFFD:C_OFFD + E * E] = j != i
    c[:, C_RESET:C_ALL] = np.arange(E * 2 * UNITS) % UNITS != 0
    return c


def xattn_moe_kernel(nc, x, ctx_in, Wg, bg, W1, W2, consts, out):
    x_rows = x.rearrange("b s d -> (b s) d")
    c_rows = ctx_in.rearrange("b s d -> (b s) d")
    out_rows = out.rearrange("b s d -> (b s) d")
    x2n_dram = nc.dram_tensor("x2n_dram", (N_TOK, D), F32, kind="Internal").ap()

    with ExitStack() as stack:
        def sem(name):
            return stack.enter_context(nc.semaphore(name))

        def keep(name, shape, dt=F32):
            return stack.enter_context(nc.sbuf_tensor(name, shape, dt))

        cst = keep("cst", [P, C_ALL])
        wg = keep("wg", [P, KD, NARROW])
        wg_e = keep("wg_e", [P, KD, E])
        bgb = keep("bgb", [P, E])
        raw = [keep(f"raw{n}", [P, 2 * HALF]) for n in range(RAW_BUFS)]
        w_hi = [keep(f"w_hi{n}", [P, 2 * HALF], F32R) for n in range(SPLIT_BUFS)]
        w_lo = [keep(f"w_lo{n}", [P, 2 * HALF], F32R) for n in range(SPLIT_BUFS)]
        logits = keep("logits", [P, UNITS, E])
        cmp_a = keep("cmp_a", [P, UNITS, E, E])
        cmp_b = keep("cmp_b", [P, UNITS, E, E])
        rank = keep("rank", [P, UNITS, E])
        assigned = keep("assigned", [P, UNITS, E])
        al = keep("al", [P, UNITS, E])
        margin = keep("margin", [P, UNITS, E])
        p_exp = keep("p_exp", [P, UNITS, E])
        p_sel = keep("p_sel", [P, UNITS, E])
        key = keep("key", [P, UNITS, E])
        key_b = keep("key_b", [P, UNITS, E])
        key_w = keep("key_w", [P, UNITS, E, WAYS])
        thr = keep("thr", [P, 1])
        low = keep("low", [P, 1])
        count = keep("count", [P, 1])
        enough = keep("enough", [P, 1])
        junk = keep("junk", [P, N_TOK], mybir.dt.bfloat16)
        lowpick = keep("lowpick", [P, E])
        t_low = keep("t_low", [P, E])
        t_high = keep("t_high", [P, E])
        mask = keep("mask", [P, E, 2, UNITS])
        ge = keep("ge", [P, E, UNITS])
        tot = keep("tot", [P, E * 2 * UNITS])
        scan = keep("scan", [P, E * 2 * UNITS])
        pre = keep("pre", [P, E, 2, UNITS])
        slot = keep("slot", [P, E, UNITS])
        slot_b = keep("slot_b", [P, E, UNITS])
        s_hi = keep("s_hi", [P, E, UNITS])
        s_c = keep("s_c", [P, E, UNITS])
        s_lo = keep("s_lo", [P, E, UNITS])
        pay = keep("pay", [P, E, UNITS, ST, 2])
        found = keep("found", [P, E, ST, 2])
        f_idx = keep("f_idx", [P, E, ST])
        f_empty = keep("f_empty", [P, E, ST])
        idx_all = keep("idx_all", [P, E, ST], U32)
        prob_all = keep("prob_all", [P, E, ST])
        credit = keep("credit", [P, 1])
        ident = cst[:, C_IDENT:C_IDENT + P]

        with ExitStack() as phase:
            def att(name, shape, dt=F32):
                return phase.enter_context(nc.sbuf_tensor(name, shape, dt))

            x_all = att("x_all", [P, UNITS, D])
            c_sb = [att(f"c_sb{n}", [P, D]) for n in range(2)]
            c_sq = att("c_sq", [P, D])
            x_norm = att("x_norm", [P, D])
            x_sq = att("x_sq", [P, D])
            k_hi = [att(f"k_hi{n}", [P, D], F32R) for n in range(2)]
            k_lo = [att(f"k_lo{n}", [P, D], F32R) for n in range(2)]
            q_f = att("q_f", [P, D])
            q_hi = [att(f"q_hi{n}", [P, D], F32R) for n in range(2)]
            q_lo = [att(f"q_lo{n}", [P, D], F32R) for n in range(2)]
            v_t = [att(f"v_t{n}", [P, TT, 4, DH]) for n in range(2)]
            prob = [[att(f"prob{h}{n}", [P, D]) for n in range(2)] for h in range(2)]
            o_sb = [att(f"o_sb{h}", [P, D]) for h in range(2)]
            o_norm = att("o_norm", [P, D])
            x2n = [att(f"x2n{n}", [P, D]) for n in range(2)]
            x2n_t = att("x2n_t", [P, KD, P])
            stats = att("stats", [P, 6])
            mv = att("mv", [P, 2])
            var_e = att("var_e", [P, 1])
            rstd = att("rstd", [P, 1])
            pad = att("pad", [P, 1])
            pad2 = att("pad2", [P, 1])
            stats2 = att("stats2", [P, 6])
            mv2 = att("mv2", [P, 2])
            var2_e = att("var2_e", [P, 1])
            rstd2 = att("rstd2", [P, 1])
            ss = att("ss", [P, 16])
            rnorm = [att(f"rnorm{n}", [P, 2, TT, 2]) for n in range(2)]
            rsum = att("rsum", [P, TT, 2])
            wide_q = att("wide_q", [P, TT, 2, DH])
            wide_s = att("wide_s", [P, TT, 2, DH])
            power = att("power", [P, 16])

        with ExitStack() as phase:
            def ffn(name, shape, dt=F32):
                return phase.enter_context(nc.sbuf_tensor(name, shape, dt))

            xt_hi = ffn("xt_hi", [P, 2, KD, CAP], F32R)
            xt_lo = ffn("xt_lo", [P, 2, KD, CAP], F32R)
            x_got = ffn("x_got", [P, ST, D])
            o_got = ffn("o_got", [P, ST, D])
            h_f = [ffn(f"h_f{n}", [P, CAP]) for n in range(2)]
            h_hi = [ffn(f"h_hi{n}", [P, CAP], F32R) for n in range(2)]
            h_lo = [ffn(f"h_lo{n}", [P, CAP], F32R) for n in range(2)]
            onehot = [ffn(f"onehot{n}", [P, UNITS, P]) for n in range(2)]

        four = stack.enter_context(nc.psum_tensor("four", [P, 4, 512], F32))
        two = [stack.enter_context(nc.psum_tensor(f"two{n}", [P, 512], F32)) for n in range(2)]
        bank_t = stack.enter_context(nc.psum_tensor("bank_t", [P, 512], F32))
        bank_m = stack.enter_context(nc.psum_tensor("bank_m", [P, 512], F32))
        s_ps, o_ps = four, two
        acc_ps, z_ps = four, two

        cst_in = sem("cst_in")
        wg_in = sem("wg_in")
        bg_in = sem("bg_in")
        wg_done = sem("wg_done")
        x_in = [sem(f"x_in{n}") for n in range(2)]
        c_in = [sem(f"c_in{n}") for n in range(2)]
        v_ones = sem("v_ones")
        power_set = sem("power_set")
        bn_done = sem("bn_done")
        mv_done = sem("mv_done")
        var_done = sem("var_done")
        rstd_done = sem("rstd_done")
        khi_done = sem("khi_done")
        k_split = sem("k_split")
        xn_done = sem("xn_done")
        csq_done = sem("csq_done")
        xsq_done = sem("xsq_done")
        ss_ready = sem("ss_ready")
        ss_taken = sem("ss_taken")
        rnorm_done = sem("rnorm_done")
        wq_done = sem("wq_done")
        rq_ready = sem("rq_ready")
        q_done = sem("q_done")
        qhi_done = sem("qhi_done")
        q_split = sem("q_split")
        v_ready = sem("v_ready")
        v_taken = sem("v_taken")
        scores_ready = sem("scores_ready")
        exp_done = sem("exp_done")
        pv_done = sem("pv_done")
        o_taken = sem("o_taken")
        sums_ready = sem("sums_ready")
        rsum_done = sem("rsum_done")
        ws_done = sem("ws_done")
        rb_ready = sem("rb_ready")
        on_done = sem("on_done")
        x2_done = sem("x2_done")
        bn2_done = sem("bn2_done")
        mv2_done = sem("mv2_done")
        var2_done = sem("var2_done")
        rstd2_done = sem("rstd2_done")
        x2n_done = sem("x2n_done")
        x2t_ready = sem("x2t_ready")
        x2t_taken = sem("x2t_taken")
        logit_ready = sem("logit_ready")
        logit_done = sem("logit_done")
        x2_stored = sem("x2_stored")
        x2n_stored = [sem(f"x2n_stored{n}") for n in range(2)]
        step = sem("step")
        e_neg = sem("e_neg")
        margin_done = sem("margin_done")
        key_done = sem("key_done")
        key_t = sem("key_t")
        enough_done = sem("enough_done")
        n_ready = sem("n_ready")
        pick_done = sem("pick_done")
        t_ready = sem("t_ready")
        mask_done = sem("mask_done")
        pre_ready = sem("pre_ready")
        pay_done = sem("pay_done")
        oh_done = sem("oh_done")
        found_ready = sem("found_ready")
        idx_done = sem("idx_done")
        got_clear = sem("got_clear")
        raw_in = [sem(f"raw_in{n}") for n in range(RAW_BUFS)]
        whi_done = sem("whi_done")
        wlo_done = sem("wlo_done")
        z_ready = sem("z_ready")
        gelu_done = sem("gelu_done")
        h_split = sem("h_split")
        x_gathered = sem("x_gathered")
        o_gathered = sem("o_gathered")
        xt_ready = sem("xt_ready")
        xthi_done = sem("xthi_done")
        xt_split = sem("xt_split")
        acc_ready = sem("acc_ready")
        y_done = sem("y_done")
        scattered = sem("scattered")

        block = stack.enter_context(nc.Block())

        def number(u):
            return 2 * u[0] + u[1]

        def after(u):
            return (u[0], 1) if u[1] == 0 else (u[0] + 1, 0)

        def before(u):
            return (u[0], 0) if u[1] == 1 else (u[0] - 1, 1)

        def run_units(engine, unit):
            last = UNITS // 2 - 1
            unit((0, 0), 0, 2)
            unit((0, 1), 1, 2)
            unit((1, 0), 2, 2)
            with engine.Fori(1, last - 1) as h:
                unit((h, 1), 3, 2)
                unit((h + 1, 0), 3, 2)
            unit((last - 1, 1), 3, 2)
            unit((last, 0), 3, 1)
            unit((last, 1), 3, 0)

        def run_experts(engine, expert):
            with engine.Fori(0, E - 1) as e:
                expert(e, False)
            expert(E - 1, True)

        def raw_halves(n):
            return (raw[n][:, 0:HALF].rearrange("p (k c) -> p k c", k=KD),
                    raw[n][:, HALF:2 * HALF].rearrange("p (m d) -> p m d", m=CHUNK_M))

        @block.sync
        def _(sp):
            def load_unit(u):
                n = number(u)
                sp.dma_start(c_sb[u[1]][:, :], c_rows[bass.ds(n * P, P), :]).then_inc(c_in[u[1]], 16)
                sp.dma_start(x_all[:, bass.ds(n, 1), :],
                             x_rows[bass.ds(n * P, P), :].rearrange("p (a d) -> p a d", a=1)
                             ).then_inc(x_in[u[1]], 16)

            def load_chunk(e, c):
                n = c % RAW_BUFS
                up, down = raw_halves(n)
                sp.dma_start(up, W1[bass.ds(e, 1), :, c * CW:(c + 1) * CW]
                             .rearrange("a (k p) c -> p (a k) c", p=P)).then_inc(raw_in[n], 16)
                sp.dma_start(down, W2[bass.ds(e, 1), c * CW:(c + 1) * CW, :]
                             .rearrange("a (m p) d -> p (a m) d", p=P)).then_inc(raw_in[n], 16)

            load_unit((0, 0))
            sp.dma_start(cst[:, :], consts).then_inc(cst_in, 16)
            load_unit((0, 1))
            sp.dma_start(wg_e[:, :, :], Wg.rearrange("(k p) e -> p k e", p=P)).then_inc(wg_in, 16)
            sp.dma_start(bgb[:, :], bg.rearrange("(a e) -> a e", a=1).broadcast_to([P, E])).then_inc(bg_in, 16)

            def store_unit(u):
                n = number(u)
                sp.wait_ge(x2_done, n + 1)
                sp.dma_start(out_rows[bass.ds(n * P, P), :].rearrange("p (a d) -> p a d", a=1),
                             x_all[:, bass.ds(n, 1), :]).then_inc(x2_stored, 16)
                sp.wait_ge(x2n_done, n + 1)
                sp.dma_start(x2n_dram[bass.ds(n * P, P), :], x2n[u[1]][:, :]).then_inc(x2n_stored[u[1]], 16)

            def load_next(u):
                n = number(u)
                sp.wait_ge(csq_done, n - 1)
                sp.wait_ge(k_split, n - 1)
                sp.wait_ge(v_ready, n - 1)
                sp.wait_ge(xn_done, n - 1)
                load_unit(u)

            for c in range(RAW_BUFS):
                load_chunk(0, c)
            load_next((1, 0))
            with sp.Fori(1, UNITS // 2 - 1) as h:
                load_next((h, 1))
                store_unit((h - 1, 0))
                load_next((h + 1, 0))
                store_unit((h - 1, 1))
            end = UNITS // 2 - 1
            load_next((end, 1))
            for u in ((end - 1, 0), (end - 1, 1), (end, 0), (end, 1)):
                store_unit(u)

            def expert(e, last):
                for c in range(CHUNKS):
                    k = c + RAW_BUFS
                    if last and k >= CHUNKS:
                        break
                    sp.wait_ge(wlo_done, e * CHUNKS + c + 1)
                    load_chunk(e if k < CHUNKS else e + 1, k % CHUNKS)

            run_experts(sp, expert)
            sp.wait_ge(x2_stored, 16 * UNITS)
            for n in range(2):
                sp.wait_ge(x2n_stored[n], 16 * UNITS // 2)
            sp.wait_ge(scattered, 16 * ST * E)

        @block.gpsimd
        def _(pool):
            def inv_sqrt(dst, src, n):
                return nc.gpsimd.tensor_tensor(dst, src, power[:, 0:n], ALU.pow)

            nc.gpsimd.memset(power[:, :], -0.5).then_inc(power_set, 1)
            for n in range(2):
                nc.gpsimd.memset(v_t[n][:, :, 1:3, :], 1.0).then_inc(v_ones, 1)
            pool.wait_ge(power_set, 1)

            def prepare(u):
                pool.wait_ge(var_done, number(u) + 1)
                inv_sqrt(rstd[:, :], var_e[:, :], 1).then_inc(rstd_done, 1)

            def norms(u):
                n = number(u)
                pool.wait_ge(ss_taken, n + 1)
                inv_sqrt(rnorm[u[1]][:, :, :, :].rearrange("p a t h -> p (a t h)"), ss[:, :], 16
                         ).then_inc(rnorm_done, 1)

            def finish(u):
                n = number(u)
                pool.wait_ge(var2_done, n + 1)
                inv_sqrt(rstd2[:, :], var2_e[:, :], 1).then_inc(rstd2_done, 1)

            prepare((0, 0))
            norms((0, 0))
            prepare((0, 1))

            def unit(u, behind, ahead):
                if ahead:
                    if behind:
                        pool.wait_ge(exp_done, TT * number(u))
                    norms(after(u))
                if behind:
                    finish(before(u))
                if ahead > 1:
                    prepare(after(after(u)))

            run_units(pool, unit)
            finish((UNITS // 2 - 1, 1))

            pool.wait_ge(logit_done, UNITS)
            pool.wait_ge(x2_stored, 16 * UNITS)
            for n in range(2):
                pool.wait_ge(x2n_stored[n], 16 * UNITS // 2)
            nc.gpsimd.memset(x_got[:, :, :], 0.0).then_inc(got_clear, 1)
            nc.gpsimd.memset(o_got[:, :, :], 0.0).then_inc(got_clear, 1)
            pool.wait_ge(got_clear, 2)
            pool.wait_ge(idx_done, 2)

            def gather_x(e):
                for t in range(ST):
                    nc.gpsimd.indirect_dma_start(
                        x_got[:, t, :], None, x2n_dram,
                        bass.IndirectOffsetOnAxis(idx_all[:, e, t:t + 1], 0),
                        bounds_check=N_TOK - 1, oob_is_err=False).then_inc(x_gathered, 16)

            gather_x(0)
            for e in range(E):
                if e + 1 < E:
                    pool.wait_ge(xt_ready, ST * (e + 1))
                    gather_x(e + 1)
                if e > 0:
                    pool.wait_ge(scattered, 16 * ST * e)
                for t in range(ST):
                    nc.gpsimd.indirect_dma_start(
                        o_got[:, t, :], None, out_rows,
                        bass.IndirectOffsetOnAxis(idx_all[:, e, t:t + 1], 0),
                        bounds_check=N_TOK - 1, oob_is_err=False).then_inc(o_gathered, 16)
                for t in range(ST):
                    pool.wait_ge(y_done, ST * (e + 1) + t + 1)
                    nc.gpsimd.indirect_dma_start(
                        out_rows, bass.IndirectOffsetOnAxis(idx_all[:, e, t:t + 1], 0), o_got[:, t, :], None,
                        bounds_check=N_TOK - 1, oob_is_err=False).then_inc(scattered, 16)

        @block.scalar
        def _(act):
            def squares(u, first):
                n = number(u)
                act.wait_ge(c_in[u[1]], 16 * (u[0] + 1))
                if not first:
                    act.wait_ge(ss_ready, n)
                nc.scalar.activation(c_sq[:, :], c_sb[u[1]][:, :], ACT.Square).then_inc(csq_done, 1)
                act.wait_ge(xn_done, n + 1)
                nc.scalar.activation(x_sq[:, :], x_norm[:, :], ACT.Square).then_inc(xsq_done, 1)

            def take_v(u, reused):
                n = number(u)
                act.wait_ge(v_ready, n + 1)
                if reused:
                    act.wait_ge(pv_done, TT * (n - 1))
                nc.scalar.activation(v_t[u[1]][:, :, 0:4:3, :],
                                     bank_t[:, :].rearrange("p (t h d) -> p t h d", t=TT, h=2),
                                     ACT.Copy).then_inc(v_taken, 1)

            def exponentials(u, t, reused):
                g = TT * number(u) + t
                act.wait_ge(scores_ready, g + 1)
                if reused:
                    act.wait_ge(pv_done, g - 1)
                for h in range(2):
                    last = nc.scalar.activation(prob[h][t % 2][:, :], s_ps[:, 2 * (t % 2) + h, :], ACT.Exp,
                                                scale=rnorm[u[1]][:, 0, t, h:h + 1])
                last.then_inc(exp_done, 1)

            def take_o(u, reused):
                n = number(u)
                act.wait_ge(pv_done, TT * (n + 1))
                if reused:
                    act.wait_ge(on_done, n)
                for h in range(2):
                    last = nc.scalar.activation(o_sb[h][:, :], o_ps[h][:, :], ACT.Copy)
                last.then_inc(o_taken, 1)

            def take_x2t(u):
                act.wait_ge(x2t_ready, number(u) + 1)
                nc.scalar.activation(x2n_t[:, :, :], bank_t[:, :].rearrange("p (k t) -> p k t", k=KD),
                                     ACT.Copy).then_inc(x2t_taken, 1)

            squares((0, 0), True)
            act.wait_ge(v_ones, 2)
            take_v((0, 0), False)
            act.wait_ge(rnorm_done, 1)

            def unit(u, behind, ahead):
                exponentials(u, 0, behind > 0)
                if ahead:
                    squares(after(u), False)
                if behind > 1:
                    take_x2t(before(before(u)))
                exponentials(u, 1, behind > 0)
                exponentials(u, 2, True)
                exponentials(u, 3, True)
                if ahead:
                    take_v(after(u), behind > 0)
                take_o(u, behind > 0)
                if ahead:
                    act.wait_ge(rnorm_done, number(u) + 2)

            run_units(act, unit)
            take_x2t((UNITS // 2 - 1, 0))
            act.wait_ge(logit_ready, UNITS - 1)
            take_x2t((UNITS // 2 - 1, 1))

            act.wait_ge(margin_done, 1)
            nc.scalar.activation(p_exp[:, :, :], margin[:, :, :], ACT.Exp, scale=-1.0).then_inc(e_neg, 1)

            def split_hi(e, c):
                act.wait_ge(raw_in[c % RAW_BUFS], 32 * ((CHUNKS // RAW_BUFS) * e + c // RAW_BUFS + 1))
                nc.scalar.activation(w_hi[c % SPLIT_BUFS][:, :], raw[c % RAW_BUFS][:, :], ACT.Copy
                                     ).then_inc(whi_done, 1)

            for c in range(AHEAD):
                split_hi(0, c)
            act.wait_ge(found_ready, E)

            def expert(e, last):
                for m in range(MT):
                    n = MT * e + m
                    act.wait_ge(z_ready, n + 1)
                    nc.scalar.activation(h_f[m % 2][:, :], z_ps[m % 2][:, :], ACT.Gelu)
                    nc.scalar.activation(h_hi[m % 2][:, :], z_ps[m % 2][:, :], ACT.Gelu).then_inc(gelu_done, 1)
                    if m % CHUNK_M == 0:
                        c = m // CHUNK_M + AHEAD
                        if c < CHUNKS:
                            split_hi(e, c)
                        elif not last:
                            split_hi(e + 1, c - CHUNKS)

            run_experts(act, expert)

        @block.vector
        def _(dve):
            def prepare(u, reused):
                n = number(u)
                xu = x_all[:, bass.ds(n, 1), :].rearrange("p a d -> p (a d)")
                dve.wait_ge(x_in[u[1]], 16 * (u[0] + 1))
                dve.wait_ge(c_in[u[1]], 16 * (u[0] + 1))
                if reused:
                    dve.wait_ge(scores_ready, TT * (n - 1))
                nc.vector.tensor_copy(k_hi[u[1]][:, :], c_sb[u[1]][:, :]).then_inc(khi_done, 1)
                nc.vector.bn_stats(stats[:, :], xu).then_inc(bn_done, 1)
                dve.wait_ge(khi_done, n + 1)
                dve.wait_ge(bn_done, n + 1)
                nc.vector.tensor_tensor(k_lo[u[1]][:, :], c_sb[u[1]][:, :], k_hi[u[1]][:, :].bitcast(F32),
                                        ALU.subtract).then_inc(k_split, 1)
                nc.vector.bn_aggr(mv[:, :], stats[:, :]).then_inc(mv_done, 1)
                dve.wait_ge(mv_done, n + 1)
                nc.vector.tensor_scalar(var_e[:, :], mv[:, 1:2], LN_EPS, None, ALU.add).then_inc(var_done, 1)
                dve.wait_ge(rstd_done, n + 1)
                nc.vector.tensor_scalar(x_norm[:, :], xu, mv[:, 0:1], rstd[:, 0:1], ALU.subtract, ALU.mult
                                        ).then_inc(xn_done, 1)

            def take_ss(u):
                dve.wait_ge(ss_ready, number(u) + 1)
                nc.vector.tensor_scalar(ss[:, :], bank_m[:, 0:512:REP], NORM_EPS2, None, ALU.max
                                        ).then_inc(ss_taken, 1)

            def take_logits(u):
                n = number(u)
                dve.wait_ge(logit_ready, n + 1)
                nc.vector.tensor_tensor(logits[:, bass.ds(n, 1), :].rearrange("p a e -> p (a e)"),
                                        bank_t[:, 0:E], bgb[:, :], ALU.add).then_inc(logit_done, 1)

            def queries(u):
                n = number(u)
                dve.wait_ge(rq_ready, n + 1)
                nc.vector.scalar_tensor_tensor(q_f[:, :], x_norm[:, :], ALPHA, bank_m[:, :], ALU.mult, ALU.mult
                                               ).then_inc(q_done, 1)
                dve.wait_ge(q_done, n + 1)
                nc.vector.tensor_copy(q_hi[u[1]][:, :], q_f[:, :]).then_inc(qhi_done, 1)
                dve.wait_ge(qhi_done, n + 1)
                nc.vector.tensor_tensor(q_lo[u[1]][:, :], q_f[:, :], q_hi[u[1]][:, :].bitcast(F32),
                                        ALU.subtract).then_inc(q_split, 1)

            def widen_queries(u):
                dve.wait_ge(rnorm_done, number(u) + 1)
                nc.vector.tensor_copy(wide_q[:, :, :, :], rnorm[u[1]][:, 1, :, :].unsqueeze(3)
                                      .broadcast_to([P, TT, 2, DH])).then_inc(wq_done, 1)

            def invert_sums(u):
                n = number(u)
                dve.wait_ge(sums_ready, n + 1)
                nc.vector.reciprocal(rsum[:, :, :].rearrange("p t h -> p (t h)"), bank_m[:, 0:512:NARROW]
                                     ).then_inc(rsum_done, 1)
                dve.wait_ge(rsum_done, n + 1)
                nc.vector.tensor_copy(wide_s[:, :, :, :], rsum[:, :, :].unsqueeze(3)
                                      .broadcast_to([P, TT, 2, DH])).then_inc(ws_done, 1)

            def residual(u, reused):
                n = number(u)
                xu = x_all[:, bass.ds(n, 1), :].rearrange("p a d -> p (a d)")
                dve.wait_ge(rb_ready, n + 1)
                nc.vector.tensor_tensor(o_norm[0:DH, :], o_sb[0][0:DH, :], bank_m[0:DH, :], ALU.mult)
                nc.vector.tensor_tensor(o_norm[DH:P, :], o_sb[1][DH:P, :], bank_m[DH:P, :], ALU.mult
                                        ).then_inc(on_done, 1)
                dve.wait_ge(on_done, n + 1)
                nc.vector.tensor_tensor(xu, xu, o_norm[:, :], ALU.add).then_inc(x2_done, 1)
                dve.wait_ge(x2_done, n + 1)
                nc.vector.memset(pad[:, :], 0.0)
                nc.vector.bn_stats(stats2[:, :], xu).then_inc(bn2_done, 1)
                dve.wait_ge(bn2_done, n + 1)
                nc.vector.memset(pad2[:, :], 0.0)
                nc.vector.bn_aggr(mv2[:, :], stats2[:, :]).then_inc(mv2_done, 1)
                dve.wait_ge(mv2_done, n + 1)
                nc.vector.tensor_scalar(var2_e[:, :], mv2[:, 1:2], LN_EPS, None, ALU.add).then_inc(var2_done, 1)
                dve.wait_ge(rstd2_done, n + 1)
                if reused:
                    dve.wait_ge(x2n_stored[u[1]], 16 * u[0])
                nc.vector.tensor_scalar(x2n[u[1]][:, :], xu, mv2[:, 0:1], rstd2[:, 0:1], ALU.subtract, ALU.mult
                                        ).then_inc(x2n_done, 1)

            dve.wait_ge(cst_in, 16)
            dve.wait_ge(bg_in, 16)
            dve.wait_ge(wg_in, 16)
            nc.vector.tensor_copy(wg[:, :, :].rearrange("p k (r e) -> p k r e", e=E),
                                  wg_e[:, :, :].unsqueeze(2).broadcast_to([P, KD, NARROW // E, E])
                                  ).then_inc(wg_done, 1)
            prepare((0, 0), False)
            take_ss((0, 0))
            widen_queries((0, 0))
            queries((0, 0))
            prepare((0, 1), False)

            def unit(u, behind, ahead):
                if ahead:
                    take_ss(after(u))
                if behind > 1:
                    take_logits(before(before(u)))
                if behind:
                    invert_sums(before(u))
                if ahead:
                    widen_queries(after(u))
                    queries(after(u))
                if behind:
                    residual(before(u), behind > 2)
                if ahead > 1:
                    prepare(after(after(u)), True)

            run_units(dve, unit)
            end = (UNITS // 2 - 1, 1)
            invert_sums(end)
            take_logits(before(end))
            residual(end, True)
            take_logits(end)

            done = [0]

            def link(ins):
                done[0] += 1
                ins.then_inc(step, 1)
                dve.wait_ge(step, done[0])

            dve.wait_ge(logit_done, UNITS)
            four_d = [P, UNITS, E, E]
            l_j = logits[:, :, :].unsqueeze(2).broadcast_to(four_d)
            l_i = logits[:, :, :].unsqueeze(3).broadcast_to(four_d)
            tie = cst[:, C_TIE:C_TIE + E * E].rearrange("p (i j) -> p i j", i=E).unsqueeze(1).broadcast_to(four_d)
            offd = cst[:, C_OFFD:C_OFFD + E * E].rearrange("p (i j) -> p i j", i=E).unsqueeze(1).broadcast_to(four_d)
            link(nc.vector.tensor_tensor(cmp_a[:, :, :, :], l_j, l_i, ALU.is_gt))
            link(nc.vector.tensor_tensor(cmp_b[:, :, :, :], l_j, l_i, ALU.is_equal))
            link(nc.vector.tensor_tensor(cmp_b[:, :, :, :], cmp_b[:, :, :, :], tie, ALU.mult))
            link(nc.vector.tensor_tensor(cmp_a[:, :, :, :], cmp_a[:, :, :, :], cmp_b[:, :, :, :], ALU.add))
            link(nc.vector.tensor_reduce(rank[:, :, :], cmp_a[:, :, :, :], AX_X, ALU.add))
            link(nc.vector.tensor_scalar(assigned[:, :, :], rank[:, :, :], 1.5, None, ALU.is_lt))
            link(nc.vector.tensor_tensor(al[:, :, :], assigned[:, :, :], logits[:, :, :], ALU.mult))
            link(nc.vector.tensor_tensor(cmp_b[:, :, :, :], al[:, :, :].unsqueeze(2).broadcast_to(four_d), offd,
                                         ALU.mult))
            link(nc.vector.tensor_reduce(rank[:, :, :], cmp_b[:, :, :, :], AX_X, ALU.add))
            nc.vector.tensor_tensor(margin[:, :, :], logits[:, :, :], rank[:, :, :], ALU.subtract
                                    ).then_inc(margin_done, 1)
            dve.wait_ge(margin_done, 1)
            link(nc.vector.tensor_scalar(key[:, :, :], margin[:, :, :], KEY_CLAMP, -KEY_CLAMP, ALU.min, ALU.max))
            link(nc.vector.tensor_scalar(key_b[:, :, :], assigned[:, :, :], -KEY_OUT, KEY_OUT, ALU.mult, ALU.add))
            link(nc.vector.tensor_tensor(key[:, :, :], key[:, :, :], assigned[:, :, :], ALU.mult))
            link(nc.vector.tensor_tensor(key[:, :, :], key[:, :, :], key_b[:, :, :], ALU.add))
            nc.vector.tensor_copy(key_w[:, :, :, :], key[:, :, :].unsqueeze(3).broadcast_to([P, UNITS, E, WAYS])
                                  ).then_inc(key_done, 1)
            link(nc.vector.memset(low[:, :], KEY_LO))
            dve.wait_ge(e_neg, 1)
            link(nc.vector.tensor_scalar(p_exp[:, :, :], p_exp[:, :, :], 1.0, None, ALU.add))
            link(nc.vector.reciprocal(p_sel[:, :, :], p_exp[:, :, :]))

            dve.wait_ge(key_t, 1)
            dve.wait_ge(key_done, 1)
            width = KEY_RANGE / WAYS
            for r in range(ROUNDS):
                link(nc.vector.tensor_scalar(thr[:, :], cst[:, C_KVEC:C_KVEC + 1], width, low[:, 0:1],
                                             ALU.mult, ALU.add))
                link(nc.vector.tensor_scalar(junk[:, :].rearrange("p (a t) -> p a t", a=4), four[:, :, :],
                                             thr[:, 0:1], None, ALU.is_ge, ALU.add, accum_out=count[:, :]))
                nc.vector.tensor_scalar(enough[:, :], count[:, :], CAP - 0.5, None, ALU.is_ge
                                        ).then_inc(enough_done, 1)
                dve.wait_ge(n_ready, r + 1)
                link(nc.vector.scalar_tensor_tensor(low[:, :], bank_m[:, 0:1], width, low[:, :],
                                                    ALU.mult, ALU.add))
                if r < ROUNDS - 1:
                    width /= WAYS
            nc.vector.tensor_scalar(lowpick[:, :], cst[:, C_PICK:C_PICK + E], low[:, 0:1], None, ALU.mult
                                    ).then_inc(pick_done, 1)
            dve.wait_ge(t_ready, 1)
            link(nc.vector.tensor_copy(t_low[:, :], bank_t[:, 0:E]))
            link(nc.vector.tensor_scalar(t_high[:, :], t_low[:, :], width, None, ALU.add))

            three_d = [P, E, UNITS]
            key_e = key[:, :, :].rearrange("p t e -> p e t")
            link(nc.vector.tensor_tensor(ge[:, :, :], key_e, t_low[:, :].unsqueeze(2).broadcast_to(three_d),
                                         ALU.is_ge))
            link(nc.vector.tensor_tensor(mask[:, :, 0, :], key_e, t_high[:, :].unsqueeze(2).broadcast_to(three_d),
                                         ALU.is_ge))
            nc.vector.tensor_tensor(mask[:, :, 1, :], ge[:, :, :], mask[:, :, 0, :], ALU.subtract
                                    ).then_inc(mask_done, 1)
            dve.wait_ge(pre_ready, 1)
            flat = E * 2 * UNITS
            pre_flat = pre[:, :, :, :].rearrange("p e g t -> p (e g t)")
            link(nc.vector.tensor_copy(tot[:, :], two[0][:, flat:2 * flat]))
            link(nc.vector.tensor_tensor_scan(scan[:, :], cst[:, C_RESET:C_RESET + flat], tot[:, :], 0.0,
                                              ALU.mult, ALU.add))
            link(nc.vector.tensor_tensor(pre_flat, two[0][:, 0:flat], scan[:, :], ALU.add))
            link(nc.vector.tensor_tensor(pre_flat, pre_flat, tot[:, :], ALU.subtract))
            above = scan[:, :].rearrange("p (e g t) -> p e g t", e=E, g=2)[:, :, 0, UNITS - 1:UNITS]
            link(nc.vector.tensor_tensor(pre[:, :, 1, :], pre[:, :, 1, :], above.broadcast_to(three_d), ALU.add))
            link(nc.vector.tensor_tensor(slot[:, :, :], mask[:, :, 0, :], pre[:, :, 0, :], ALU.mult))
            link(nc.vector.tensor_tensor(slot_b[:, :, :], mask[:, :, 1, :], pre[:, :, 1, :], ALU.mult))
            link(nc.vector.tensor_tensor(slot[:, :, :], slot[:, :, :], slot_b[:, :, :], ALU.add))
            link(nc.vector.tensor_scalar(s_c[:, :, :], ge[:, :, :], -NO_SLOT, NO_SLOT, ALU.mult, ALU.add))
            link(nc.vector.tensor_tensor(slot[:, :, :], slot[:, :, :], s_c[:, :, :], ALU.add))
            link(nc.vector.tensor_scalar(s_hi[:, :, :], slot[:, :, :], float(P), None, ALU.is_ge))
            for s in range(2, ST):
                link(nc.vector.scalar_tensor_tensor(s_hi[:, :, :], slot[:, :, :], float(s * P), s_hi[:, :, :],
                                                    ALU.is_ge, ALU.add))
            link(nc.vector.scalar_tensor_tensor(s_lo[:, :, :], s_hi[:, :, :], -float(P), slot[:, :, :],
                                                ALU.mult, ALU.add))
            tok = cst[:, C_TOK:C_TOK + UNITS].unsqueeze(1).broadcast_to(three_d)
            for s in range(ST):
                link(nc.vector.scalar_tensor_tensor(pay[:, :, :, s, 0], s_hi[:, :, :], float(s), tok,
                                                    ALU.is_equal, ALU.mult))
                link(nc.vector.scalar_tensor_tensor(pay[:, :, :, s, 1], s_hi[:, :, :], float(s),
                                                    p_sel[:, :, :].rearrange("p t e -> p e t"),
                                                    ALU.is_equal, ALU.mult))
            dve.wait_ge(x2_stored, 16 * UNITS)
            for n in range(2):
                dve.wait_ge(x2n_stored[n], 16 * UNITS // 2)
            oh_d = [P, UNITS, P]
            for e in range(E):
                if e >= 2:
                    dve.wait_ge(found_ready, e - 1)
                nc.vector.tensor_tensor(onehot[e % 2][:, :, :],
                                        cst[:, C_IOTA:C_IOTA + P].unsqueeze(1).broadcast_to(oh_d),
                                        s_lo[:, e, :].unsqueeze(2).broadcast_to(oh_d), ALU.is_equal
                                        ).then_inc(oh_done, 1)
            dve.wait_ge(found_ready, E)
            link(nc.vector.tensor_copy(found[:, :, :, :].rearrange("p e s c -> p (e s c)"),
                                       two[1][:, 0:E * ST * 2]))
            link(nc.vector.tensor_scalar(f_empty[:, :, :], found[:, :, :, 0], 0.0, 2.0 * N_TOK,
                                         ALU.is_equal, ALU.mult))
            nc.vector.tensor_copy(prob_all[:, :, :], found[:, :, :, 1]).then_inc(idx_done, 1)
            link(nc.vector.tensor_tensor(f_idx[:, :, :], found[:, :, :, 0], f_empty[:, :, :], ALU.add))
            nc.vector.tensor_scalar(idx_all[:, :, :], f_idx[:, :, :], -1.0, None, ALU.add).then_inc(idx_done, 1)

            nc.vector.memset(credit[:, :], 0.0).then_inc(y_done, ST)

            def split_lo(e, c):
                n = CHUNKS * e + c
                dve.wait_ge(whi_done, n + 1)
                nc.vector.tensor_tensor(w_lo[c % SPLIT_BUFS][:, :], raw[c % RAW_BUFS][:, :],
                                        w_hi[c % SPLIT_BUFS][:, :].bitcast(F32), ALU.subtract
                                        ).then_inc(wlo_done, 1)

            def split_tokens(e, t, parity):
                g = ST * e + t
                bank = (bank_t, bank_m)[t % 2][:, :].rearrange("p (a k t) -> p a k t", a=1, k=KD)
                hi = xt_hi[:, bass.ds(parity, 1), :, t * P:(t + 1) * P]
                lo = xt_lo[:, bass.ds(parity, 1), :, t * P:(t + 1) * P]
                dve.wait_ge(xt_ready, g + 1)
                nc.vector.tensor_copy(hi, bank).then_inc(xthi_done, 1)
                dve.wait_ge(xthi_done, g + 1)
                nc.vector.tensor_tensor(lo, bank, hi.bitcast(F32), ALU.subtract).then_inc(xt_split, 1)

            split_lo(0, 0)
            for t in range(ST):
                split_tokens(0, t, 0)
            for c in range(1, AHEAD):
                split_lo(0, c)

            def expert(e, last):
                for m in range(MT):
                    dve.wait_ge(gelu_done, MT * e + m + 1)
                    nc.vector.tensor_tensor(h_lo[m % 2][:, :], h_f[m % 2][:, :], h_hi[m % 2][:, :].bitcast(F32),
                                            ALU.subtract).then_inc(h_split, 1)
                    if m % CHUNK_M == 0:
                        c = m // CHUNK_M + AHEAD
                        if c < CHUNKS:
                            split_lo(e, c)
                        elif not last:
                            split_lo(e + 1, c - CHUNKS)
                    if not last and XT_AT <= m < XT_AT + ST:
                        split_tokens(e + 1, m - XT_AT, (e + 1) % 2)
                dve.wait_ge(o_gathered, 16 * ST * (e + 1))
                for t in range(ST):
                    dve.wait_ge(acc_ready, ST * e + t + 1)
                    nc.vector.scalar_tensor_tensor(o_got[:, t, :], acc_ps[:, t, :], prob_all[:, bass.ds(e, 1), t],
                                                   o_got[:, t, :], ALU.mult, ALU.add).then_inc(y_done, 1)

            run_experts(dve, expert)

        @block.tensor
        def _(pe):
            def squared_norms(u):
                n = number(u)
                pe.wait_ge(csq_done, n + 1)
                pe.wait_ge(xsq_done, n + 1)
                for kind, squares in enumerate((c_sq, x_sq)):
                    for t in range(TT):
                        col = NARROW * (TT * kind + t)
                        last = nc.tensor.matmul(bank_m[:, col:col + NARROW], squares[:, t * P:(t + 1) * P],
                                                cst[:, C_HEAD:C_HEAD + NARROW], start=True, stop=True)
                last.then_inc(ss_ready, 1)

            def values(u):
                for t in range(TT):
                    last = nc.tensor.transpose(bank_t[:, t * P:(t + 1) * P], c_sb[u[1]][:, t * P:(t + 1) * P],
                                               ident)
                last.then_inc(v_ready, 1)

            def spread(wide, spread_ready):
                for t in range(TT):
                    last = nc.tensor.transpose(bank_m[:, t * P:(t + 1) * P],
                                               wide[:, t, :, :].rearrange("p h d -> p (h d)"), ident)
                last.then_inc(spread_ready, 1)

            def spread_queries(u):
                pe.wait_ge(wq_done, number(u) + 1)
                spread(wide_q, rq_ready)

            def scores(u, t, reused):
                if reused:
                    pe.wait_ge(exp_done, TT * number(u) + t - 1)
                for term, (k, q) in enumerate(((k_hi, q_hi), (k_hi, q_lo), (k_lo, q_hi))):
                    for h in range(2):
                        ch = slice(DH * h, DH * (h + 1))
                        last = nc.tensor.matmul(s_ps[:, 2 * (t % 2) + h, :], k[u[1]][ch, t * P:(t + 1) * P],
                                                q[u[1]][ch, :], start=(term == 0), stop=(term == 2))
                last.then_inc(scores_ready, 1)

            def weighted_values(u, t):
                pe.wait_ge(exp_done, TT * number(u) + t + 1)
                for h in range(2):
                    last = nc.tensor.matmul(o_ps[h][:, :], v_t[u[1]][:, t, 2 * h:2 * h + 2, :]
                                            .rearrange("p a d -> p (a d)"), prob[h][t % 2][:, :],
                                            start=(t == 0), stop=(t == TT - 1))
                last.then_inc(pv_done, 1)

            def sums(u):
                pe.wait_ge(o_taken, number(u) + 1)
                for h in range(2):
                    pick_row = cst[:, C_ROWS + h * NARROW:C_ROWS + (h + 1) * NARROW]
                    for t in range(TT):
                        col = NARROW * (2 * t + h)
                        last = nc.tensor.matmul(bank_m[:, col:col + NARROW],
                                                o_sb[h][:, t * P:(t + 1) * P], pick_row, start=True, stop=True)
                last.then_inc(sums_ready, 1)

            def spread_sums(u):
                pe.wait_ge(ws_done, number(u) + 1)
                spread(wide_s, rb_ready)

            def transpose_x2(u):
                pe.wait_ge(x2n_done, number(u) + 1)
                for k in range(KD):
                    last = nc.tensor.transpose(bank_t[:, k * P:(k + 1) * P], x2n[u[1]][:, k * P:(k + 1) * P],
                                               ident)
                last.then_inc(x2t_ready, 1)

            def router_logits(u):
                pe.wait_ge(x2t_taken, number(u) + 1)
                for k in range(KD):
                    last = nc.tensor.matmul(bank_t[:, 0:NARROW], x2n_t[:, k, :], wg[:, k, :],
                                            start=(k == 0), stop=(k == KD - 1))
                last.then_inc(logit_ready, 1)

            pe.wait_ge(cst_in, 16)
            pe.wait_ge(wg_done, 1)
            squared_norms((0, 0))
            values((0, 0))
            pe.wait_ge(ss_taken, 1)
            spread_queries((0, 0))
            pe.wait_ge(q_split, 1)
            pe.wait_ge(k_split, 1)
            scores((0, 0), 0, False)

            def unit(u, behind, ahead):
                n = number(u)
                scores(u, 1, behind > 0)
                pe.wait_ge(v_taken, n + 1)
                if behind:
                    pe.wait_ge(o_taken, n)
                weighted_values(u, 0)
                if behind > 1:
                    transpose_x2(before(before(u)))
                if ahead:
                    if behind > 1:
                        pe.wait_ge(on_done, n - 1)
                    else:
                        pe.wait_ge(q_done, n + 1)
                    squared_norms(after(u))
                scores(u, 2, True)
                if behind > 1:
                    router_logits(before(before(u)))
                weighted_values(u, 1)
                if behind:
                    if ahead:
                        pe.wait_ge(ss_taken, n + 2)
                    sums(before(u))
                scores(u, 3, True)
                if ahead:
                    if behind:
                        pe.wait_ge(rsum_done, n)
                    spread_queries(after(u))
                weighted_values(u, 2)
                if ahead:
                    if behind > 1:
                        pe.wait_ge(logit_done, n - 1)
                    values(after(u))
                if behind:
                    if ahead:
                        pe.wait_ge(q_done, n + 2)
                    spread_sums(before(u))
                weighted_values(u, 3)
                if ahead:
                    pe.wait_ge(q_split, n + 2)
                    pe.wait_ge(k_split, n + 2)
                    scores(after(u), 0, True)

            run_units(pe, unit)
            end = (UNITS // 2 - 1, 1)
            pe.wait_ge(on_done, UNITS - 1)
            sums(end)
            pe.wait_ge(logit_done, UNITS - 2)
            transpose_x2(before(end))
            pe.wait_ge(rsum_done, UNITS)
            spread_sums(end)
            router_logits(before(end))
            pe.wait_ge(logit_done, UNITS - 1)
            transpose_x2(end)
            router_logits(end)

            pe.wait_ge(key_done, 1)
            for t in range(UNITS):
                last = nc.tensor.transpose(four[:, t // 4, (t % 4) * P:(t % 4 + 1) * P],
                                           key_w[:, t, :, :].rearrange("p e w -> p (e w)"), ident)
            last.then_inc(key_t, 1)
            for r in range(ROUNDS):
                pe.wait_ge(enough_done, r + 1)
                nc.tensor.matmul(bank_m[:, 0:1], cst[:, C_BLOCK:C_BLOCK + P], enough[:, :], start=True, stop=True
                                 ).then_inc(n_ready, 1)
            pe.wait_ge(pick_done, 1)
            nc.tensor.matmul(bank_t[:, 0:E], cst[:, C_ONES:C_ONES + P], lowpick[:, :], start=True, stop=True
                             ).then_inc(t_ready, 1)
            pe.wait_ge(mask_done, 1)
            flat = E * 2 * UNITS
            mask_flat = mask[:, :, :, :].rearrange("p e g t -> p (e g t)")
            nc.tensor.matmul(two[0][:, 0:flat], cst[:, C_TRI:C_TRI + P], mask_flat, start=True, stop=True)
            nc.tensor.matmul(two[0][:, flat:2 * flat], cst[:, C_ONES:C_ONES + P], mask_flat, start=True,
                             stop=True).then_inc(pre_ready, 1)
            for e in range(E):
                pe.wait_ge(oh_done, e + 1)
                for t in range(UNITS):
                    last = nc.tensor.matmul(two[1][:, e * ST * 2:(e + 1) * ST * 2], onehot[e % 2][:, t, :],
                                            pay[:, e, t, :, :].rearrange("p s c -> p (s c)"),
                                            start=(t == 0), stop=(t == UNITS - 1))
                last.then_inc(found_ready, 1)

            def transpose_tokens(t):
                bank = (bank_t, bank_m)[t % 2]
                for k in range(KD):
                    last = nc.tensor.transpose(bank[:, k * P:(k + 1) * P], x_got[:, t, k * P:(k + 1) * P], ident)
                last.then_inc(xt_ready, 1)

            def up(e, m, parity):
                pe.wait_ge(wlo_done, CHUNKS * e + m // CHUNK_M + 1)
                c, z = (m // CHUNK_M) % SPLIT_BUFS, z_ps[m % 2]
                for k in range(KD):
                    w = slice(k * CW + (m % CHUNK_M) * P, k * CW + (m % CHUNK_M + 1) * P)
                    x_h = xt_hi[:, bass.ds(parity, 1), k, :].rearrange("p a t -> p (a t)")
                    x_l = xt_lo[:, bass.ds(parity, 1), k, :].rearrange("p a t -> p (a t)")
                    nc.tensor.matmul(z[:, :], w_hi[c][:, w], x_h, start=(k == 0), stop=False)
                    nc.tensor.matmul(z[:, :], w_hi[c][:, w], x_l, start=False, stop=False)
                    last = nc.tensor.matmul(z[:, :], w_lo[c][:, w], x_h, start=False, stop=(k == KD - 1))
                last.then_inc(z_ready, 1)

            def down(e, m):
                c = (m // CHUNK_M) % SPLIT_BUFS
                w = slice(HALF + (m % CHUNK_M) * D, HALF + (m % CHUNK_M + 1) * D)
                pe.wait_ge(h_split, MT * e + m + 1)
                for t in range(ST):
                    if m == 0:
                        pe.wait_ge(y_done, ST * e + t + 1)
                    h = slice(t * P, (t + 1) * P)
                    nc.tensor.matmul(acc_ps[:, t, :], h_hi[m % 2][:, h], w_hi[c][:, w],
                                     start=(m == 0), stop=False)
                    nc.tensor.matmul(acc_ps[:, t, :], h_hi[m % 2][:, h], w_lo[c][:, w], start=False, stop=False)
                    last = nc.tensor.matmul(acc_ps[:, t, :], h_lo[m % 2][:, h], w_hi[c][:, w], start=False,
                                            stop=(m == MT - 1))
                    if m == MT - 1:
                        last.then_inc(acc_ready, 1)

            pe.wait_ge(x_gathered, 16 * ST)
            for t in range(ST):
                if t >= 2:
                    pe.wait_ge(xt_split, t - 1)
                transpose_tokens(t)
            pe.wait_ge(xt_split, ST)
            up(0, 0, 0)

            def expert(e, last):
                for m in range(MT):
                    if m < MT - 1:
                        up(e, m + 1, e % 2)
                    elif not last:
                        pe.wait_ge(xt_split, ST * (e + 2))
                        up(e + 1, 0, (e + 1) % 2)
                    down(e, m)
                    if not last and XT_AT <= m < XT_AT + ST:
                        if m == XT_AT:
                            pe.wait_ge(x_gathered, 16 * ST * (e + 2))
                        pe.wait_ge(xt_split, ST * (e + 1) + m - XT_AT - 1)
                        transpose_tokens(m - XT_AT)

            run_experts(pe, expert)


_INS = ["x", "ctx_2048", "L0_ffn_Wg", "L0_ffn_bg", "L0_ffn_W1", "L0_ffn_W2"]


def kernel(**inputs):
    import concourse.bacc as bacc
    import numpy as np
    from concourse.bass_utils import run_bass_kernel_spmd

    nc = bacc.Bacc("TRN2", target_bir_lowering=False, num_devices=1)
    arrays, args = {}, []
    for name, a in [(n, np.ascontiguousarray(inputs[n])) for n in _INS] + [("consts", constants())]:
        arrays[f"in_{name}"] = a
        args.append(nc.dram_tensor(f"in_{name}", a.shape, F32, kind="ExternalInput").ap())
    out = nc.dram_tensor("out_0", (B, S, D), F32, kind="ExternalOutput").ap()
    xattn_moe_kernel(nc, *args, out)
    r = run_bass_kernel_spmd(nc, [arrays], core_ids=[0])
    return r.results[0]["out_0"]
```

```python
from contextlib import ExitStack

import concourse.bass as bass
from concourse import mybir

F32 = mybir.dt.float32
F32R = mybir.dt.float32r
I32 = mybir.dt.int32
U32 = mybir.dt.uint32
ALU = mybir.AluOpType
ACT = mybir.ActivationFunctionType
AX_X = mybir.AxisListType.X

P = 128
B, S, D = 4, 512, 512
HEADS = 8
DH = S // HEADS
ALPHA = 5.0
NORM_EPS2 = 1e-24
LN_EPS = 1e-5
N_TOK = B * S
UNITS = N_TOK // P
TT = D // P
E, H = 4, 2048
CAP = N_TOK // E
ST = CAP // P
KD = D // P
MT = H // P
CHUNK_M = 2
CHUNKS = MT // CHUNK_M
RAW_BUFS, SPLIT_BUFS = 2, 4
AHEAD = 2
XT_AT = 8
CW = CHUNK_M * P
HALF = KD * CW

KEY_LO, KEY_RANGE, WAYS, ROUNDS = -17.0, 34.0, 32, 6
KEY_CLAMP = 16.64
KEY_OUT = -64.0
NO_SLOT = 4096.0

NARROW = 64
REP = NARROW // 2

C_IDENT, C_TRI, C_ONES, C_BLOCK, C_IOTA = (P * n for n in range(5))
C_HEAD = 5 * P
C_ROWS = C_HEAD + NARROW
C_KVEC = C_ROWS + 2 * NARROW
C_PICK = C_KVEC + 2
C_TOK = C_PICK + E
C_TIE = C_TOK + UNITS
C_OFFD = C_TIE + E * E
C_RESET = C_OFFD + E * E
C_ALL = C_RESET + E * 2 * UNITS


def constants():
    import numpy as np

    c = np.zeros((P, C_ALL), np.float32)
    p = np.arange(P)
    c[:, C_IDENT:C_IDENT + P] = np.eye(P)
    c[:, C_TRI:C_TRI + P] = p[:, None] < p[None, :]
    c[:, C_ONES:C_ONES + P] = 1
    c[:, C_BLOCK:C_BLOCK + P] = p[:, None] // WAYS == p[None, :] // WAYS
    c[:, C_IOTA:C_IOTA + P] = p[None, :]
    c[:, C_HEAD:C_HEAD + NARROW] = p[:, None] // DH == np.arange(NARROW)[None, :] // REP
    c[DH, C_ROWS:C_ROWS + NARROW] = 1
    c[0, C_ROWS + NARROW:C_ROWS + 2 * NARROW] = 1
    c[:, C_KVEC] = p % WAYS + 1
    c[:, C_PICK:C_PICK + E] = p[:, None] == WAYS * np.arange(E)[None, :]
    c[:, C_TOK:C_TOK + UNITS] = p[:, None] + P * np.arange(UNITS)[None, :] + 1
    i, j = np.divmod(np.arange(E * E), E)
    c[:, C_TIE:C_TIE + E * E] = j < i
    c[:, C_OFFD:C_OFFD + E * E] = j != i
    c[:, C_RESET:C_ALL] = np.arange(E * 2 * UNITS) % UNITS != 0
    return c


def xattn_moe_kernel(nc, x, ctx_in, Wg, bg, W1, W2, consts, out):
    x_rows = x.rearrange("b s d -> (b s) d")
    c_rows = ctx_in.rearrange("b s d -> (b s) d")
    out_rows = out.rearrange("b s d -> (b s) d")
    x2n_dram = nc.dram_tensor("x2n_dram", (N_TOK, D), F32, kind="Internal").ap()

    with ExitStack() as stack:
        def sem(name):
            return stack.enter_context(nc.semaphore(name))

        def keep(name, shape, dt=F32):
            return stack.enter_context(nc.sbuf_tensor(name, shape, dt))

        cst = keep("cst", [P, C_ALL])
        wg = keep("wg", [P, KD, NARROW])
        wg_e = keep("wg_e", [P, KD, E])
        bgb = keep("bgb", [P, E])
        raw = [keep(f"raw{n}", [P, 2 * HALF]) for n in range(RAW_BUFS)]
        w_hi = [keep(f"w_hi{n}", [P, 2 * HALF], F32R) for n in range(SPLIT_BUFS)]
        w_lo = [keep(f"w_lo{n}", [P, 2 * HALF], F32R) for n in range(SPLIT_BUFS)]
        logits = keep("logits", [P, UNITS, E])
        cmp_a = keep("cmp_a", [P, UNITS, E, E])
        cmp_b = keep("cmp_b", [P, UNITS, E, E])
        rank = keep("rank", [P, UNITS, E])
        assigned = keep("assigned", [P, UNITS, E])
        al = keep("al", [P, UNITS, E])
        margin = keep("margin", [P, UNITS, E])
        p_exp = keep("p_exp", [P, UNITS, E])
        p_sel = keep("p_sel", [P, UNITS, E])
        key = keep("key", [P, UNITS, E])
        key_b = keep("key_b", [P, UNITS, E])
        key_w = keep("key_w", [P, UNITS, E, WAYS])
        thr = keep("thr", [P, 1])
        low = keep("low", [P, 1])
        count = keep("count", [P, 1])
        enough = keep("enough", [P, 1])
        junk = keep("junk", [P, N_TOK], mybir.dt.bfloat16)
        lowpick = keep("lowpick", [P, E])
        t_low = keep("t_low", [P, E])
        t_high = keep("t_high", [P, E])
        mask = keep("mask", [P, E, 2, UNITS])
        ge = keep("ge", [P, E, UNITS])
        tot = keep("tot", [P, E * 2 * UNITS])
        scan = keep("scan", [P, E * 2 * UNITS])
        pre = keep("pre", [P, E, 2, UNITS])
        slot = keep("slot", [P, E, UNITS])
        slot_b = keep("slot_b", [P, E, UNITS])
        s_hi = keep("s_hi", [P, E, UNITS])
        s_c = keep("s_c", [P, E, UNITS])
        s_lo = keep("s_lo", [P, E, UNITS])
        pay = keep("pay", [P, E, UNITS, ST, 2])
        found = keep("found", [P, E, ST, 2])
        f_idx = keep("f_idx", [P, E, ST])
        f_empty = keep("f_empty", [P, E, ST])
        idx_all = keep("idx_all", [P, E, ST], U32)
        prob_all = keep("prob_all", [P, E, ST])
        credit = keep("credit", [P, 1])
        ident = cst[:, C_IDENT:C_IDENT + P]

        with ExitStack() as phase:
            def att(name, shape, dt=F32):
                return phase.enter_context(nc.sbuf_tensor(name, shape, dt))

            x_all = att("x_all", [P, UNITS, D])
            c_sb = [att(f"c_sb{n}", [P, D]) for n in range(2)]
            c_sq = att("c_sq", [P, D])
            x_norm = att("x_norm", [P, D])
            x_sq = att("x_sq", [P, D])
            k_hi = [att(f"k_hi{n}", [P, D], F32R) for n in range(2)]
            k_lo = [att(f"k_lo{n}", [P, D], F32R) for n in range(2)]
            q_f = att("q_f", [P, D])
            q_hi = [att(f"q_hi{n}", [P, D], F32R) for n in range(2)]
            q_lo = [att(f"q_lo{n}", [P, D], F32R) for n in range(2)]
            v_t = [att(f"v_t{n}", [P, TT, 4, DH]) for n in range(2)]
            prob = [[att(f"prob{h}{n}", [P, D]) for n in range(2)] for h in range(2)]
            o_sb = att("o_sb", [P, D])
            p_sum = att("p_sum", [P, D])
            p_inv = att("p_inv", [P, D])
            o_norm = att("o_norm", [P, D])
            x2n = [att(f"x2n{n}", [P, D]) for n in range(2)]
            x2n_t = att("x2n_t", [P, KD, P])
            stats = att("stats", [P, 6])
            mv = att("mv", [P, 2])
            var_e = att("var_e", [P, 1])
            rstd = att("rstd", [P, 1])
            pad = att("pad", [P, 1])
            pad2 = att("pad2", [P, 1])
            stats2 = att("stats2", [P, 6])
            mv2 = att("mv2", [P, 2])
            var2_e = att("var2_e", [P, 1])
            rstd2 = att("rstd2", [P, 1])
            ss = att("ss", [P, 16])
            ss_max = att("ss_max", [P, 16])
            rnorm = [att(f"rnorm{n}", [P, 2, TT, 2]) for n in range(2)]
            wide_q = att("wide_q", [P, TT, 2, DH])
            power = att("power", [P, 16])

        with ExitStack() as phase:
            def ffn(name, shape, dt=F32):
                return phase.enter_context(nc.sbuf_tensor(name, shape, dt))

            xt_hi = ffn("xt_hi", [P, 2, KD, CAP], F32R)
            xt_lo = ffn("xt_lo", [P, 2, KD, CAP], F32R)
            x_got = ffn("x_got", [P, ST, D])
            o_got = ffn("o_got", [P, ST, D])
            h_f = [ffn(f"h_f{n}", [P, CAP]) for n in range(2)]
            h_hi = [ffn(f"h_hi{n}", [P, CAP], F32R) for n in range(2)]
            h_lo = [ffn(f"h_lo{n}", [P, CAP], F32R) for n in range(2)]
            onehot = [ffn(f"onehot{n}", [P, UNITS, P]) for n in range(2)]

        four = stack.enter_context(nc.psum_tensor("four", [P, 4, 512], F32))
        two = [stack.enter_context(nc.psum_tensor(f"two{n}", [P, 512], F32)) for n in range(2)]
        bank_t = stack.enter_context(nc.psum_tensor("bank_t", [P, 512], F32))
        bank_m = stack.enter_context(nc.psum_tensor("bank_m", [P, 512], F32))
        s_ps, o_ps = four, two
        acc_ps, z_ps = four, two

        cst_in = sem("cst_in")
        wg_in = sem("wg_in")
        bg_in = sem("bg_in")
        wg_done = sem("wg_done")
        x_in = [sem(f"x_in{n}") for n in range(2)]
        c_in = [sem(f"c_in{n}") for n in range(2)]
        v_ones = sem("v_ones")
        power_set = sem("power_set")
        bn_done = sem("bn_done")
        mv_done = sem("mv_done")
        var_done = sem("var_done")
        rstd_done = sem("rstd_done")
        khi_done = sem("khi_done")
        k_split = sem("k_split")
        xn_done = sem("xn_done")
        csq_done = sem("csq_done")
        xsq_done = sem("xsq_done")
        xt_done = sem("xt_done")
        ssq_done = sem("ssq_done")
        ssk_done = sem("ssk_done")
        ss_done = sem("ss_done")
        rnorm_done = sem("rnorm_done")
        wq_done = sem("wq_done")
        rq_ready = sem("rq_ready")
        q_done = sem("q_done")
        qhi_done = sem("qhi_done")
        q_split = sem("q_split")
        v_ready = sem("v_ready")
        v_taken = sem("v_taken")
        scores_ready = sem("scores_ready")
        exp_done = sem("exp_done")
        pv_done = sem("pv_done")
        sum_taken = sem("sum_taken")
        o_taken = sem("o_taken")
        inv_done = sem("inv_done")
        on_done = sem("on_done")
        x2_done = sem("x2_done")
        bn2_done = sem("bn2_done")
        mv2_done = sem("mv2_done")
        var2_done = sem("var2_done")
        rstd2_done = sem("rstd2_done")
        x2n_done = sem("x2n_done")
        x2t_ready = sem("x2t_ready")
        x2t_taken = sem("x2t_taken")
        logit_ready = sem("logit_ready")
        logit_done = sem("logit_done")
        x2_stored = sem("x2_stored")
        x2n_stored = [sem(f"x2n_stored{n}") for n in range(2)]
        step = sem("step")
        e_neg = sem("e_neg")
        margin_done = sem("margin_done")
        key_done = sem("key_done")
        key_t = sem("key_t")
        enough_done = sem("enough_done")
        n_ready = sem("n_ready")
        pick_done = sem("pick_done")
        t_ready = sem("t_ready")
        mask_done = sem("mask_done")
        pre_ready = sem("pre_ready")
        pay_done = sem("pay_done")
        oh_done = sem("oh_done")
        found_ready = sem("found_ready")
        idx_done = sem("idx_done")
        got_clear = sem("got_clear")
        raw_in = [sem(f"raw_in{n}") for n in range(RAW_BUFS)]
        whi_done = sem("whi_done")
        wlo_done = sem("wlo_done")
        z_ready = sem("z_ready")
        gelu_done = sem("gelu_done")
        h_split = sem("h_split")
        x_gathered = sem("x_gathered")
        o_gathered = sem("o_gathered")
        xt_ready = sem("xt_ready")
        xthi_done = sem("xthi_done")
        xt_split = sem("xt_split")
        acc_ready = sem("acc_ready")
        y_done = sem("y_done")
        scattered = sem("scattered")

        block = stack.enter_context(nc.Block())

        def number(u):
            return 2 * u[0] + u[1]

        def after(u):
            return (u[0], 1) if u[1] == 0 else (u[0] + 1, 0)

        def before(u):
            return (u[0], 0) if u[1] == 1 else (u[0] - 1, 1)

        def run_units(engine, unit):
            last = UNITS // 2 - 1
            unit((0, 0), 0, 2)
            unit((0, 1), 1, 2)
            unit((1, 0), 2, 2)
            with engine.Fori(1, last - 1) as h:
                unit((h, 1), 3, 2)
                unit((h + 1, 0), 3, 2)
            unit((last - 1, 1), 3, 2)
            unit((last, 0), 3, 1)
            unit((last, 1), 3, 0)

        def run_experts(engine, expert):
            with engine.Fori(0, E - 1) as e:
                expert(e, False)
            expert(E - 1, True)

        def raw_halves(n):
            return (raw[n][:, 0:HALF].rearrange("p (k c) -> p k c", k=KD),
                    raw[n][:, HALF:2 * HALF].rearrange("p (m d) -> p m d", m=CHUNK_M))

        @block.sync
        def _(sp):
            def load_unit(u):
                n = number(u)
                sp.dma_start(c_sb[u[1]][:, :], c_rows[bass.ds(n * P, P), :]).then_inc(c_in[u[1]], 16)
                sp.dma_start(x_all[:, bass.ds(n, 1), :],
                             x_rows[bass.ds(n * P, P), :].rearrange("p (a d) -> p a d", a=1)
                             ).then_inc(x_in[u[1]], 16)

            def load_chunk(e, c):
                n = c % RAW_BUFS
                up, down = raw_halves(n)
                sp.dma_start(up, W1[bass.ds(e, 1), :, c * CW:(c + 1) * CW]
                             .rearrange("a (k p) c -> p (a k) c", p=P)).then_inc(raw_in[n], 16)
                sp.dma_start(down, W2[bass.ds(e, 1), c * CW:(c + 1) * CW, :]
                             .rearrange("a (m p) d -> p (a m) d", p=P)).then_inc(raw_in[n], 16)

            load_unit((0, 0))
            sp.dma_start(cst[:, :], consts).then_inc(cst_in, 16)
            load_unit((0, 1))
            sp.dma_start(wg_e[:, :, :], Wg.rearrange("(k p) e -> p k e", p=P)).then_inc(wg_in, 16)
            sp.dma_start(bgb[:, :], bg.rearrange("(a e) -> a e", a=1).broadcast_to([P, E])).then_inc(bg_in, 16)

            def store_unit(u):
                n = number(u)
                sp.wait_ge(x2_done, n + 1)
                sp.dma_start(out_rows[bass.ds(n * P, P), :].rearrange("p (a d) -> p a d", a=1),
                             x_all[:, bass.ds(n, 1), :]).then_inc(x2_stored, 16)
                sp.wait_ge(x2n_done, n + 1)
                sp.dma_start(x2n_dram[bass.ds(n * P, P), :], x2n[u[1]][:, :]).then_inc(x2n_stored[u[1]], 16)

            def load_next(u):
                n = number(u)
                sp.wait_ge(k_split, n - 1)
                sp.wait_ge(v_ready, n - 1)
                sp.wait_ge(xn_done, n - 1)
                load_unit(u)

            for c in range(RAW_BUFS):
                load_chunk(0, c)
            load_next((1, 0))
            with sp.Fori(1, UNITS // 2 - 1) as h:
                load_next((h, 1))
                store_unit((h - 1, 0))
                load_next((h + 1, 0))
                store_unit((h - 1, 1))
            end = UNITS // 2 - 1
            load_next((end, 1))
            for u in ((end - 1, 0), (end - 1, 1), (end, 0), (end, 1)):
                store_unit(u)

            def expert(e, last):
                for c in range(CHUNKS):
                    k = c + RAW_BUFS
                    if last and k >= CHUNKS:
                        break
                    sp.wait_ge(wlo_done, e * CHUNKS + c + 1)
                    load_chunk(e if k < CHUNKS else e + 1, k % CHUNKS)

            run_experts(sp, expert)
            sp.wait_ge(x2_stored, 16 * UNITS)
            for n in range(2):
                sp.wait_ge(x2n_stored[n], 16 * UNITS // 2)
            sp.wait_ge(scattered, 16 * ST * E)

        @block.gpsimd
        def _(pool):
            def inv_sqrt(dst, src, n):
                return nc.gpsimd.tensor_tensor(dst, src, power[:, 0:n], ALU.pow)

            nc.gpsimd.memset(power[:, :], -0.5).then_inc(power_set, 1)
            for n in range(2):
                nc.gpsimd.memset(v_t[n][:, :, 1:3, :], 1.0).then_inc(v_ones, 1)
            pool.wait_ge(power_set, 1)

            def prepare(u):
                pool.wait_ge(var_done, number(u) + 1)
                inv_sqrt(rstd[:, :], var_e[:, :], 1).then_inc(rstd_done, 1)

            def norms(u):
                n = number(u)
                pool.wait_ge(ss_done, n + 1)
                inv_sqrt(rnorm[u[1]][:, :, :, :].rearrange("p a t h -> p (a t h)"), ss_max[:, :], 16
                         ).then_inc(rnorm_done, 1)

            def finish(u):
                n = number(u)
                pool.wait_ge(var2_done, n + 1)
                inv_sqrt(rstd2[:, :], var2_e[:, :], 1).then_inc(rstd2_done, 1)

            prepare((0, 0))
            prepare((0, 1))
            norms((0, 0))

            def unit(u, behind, ahead):
                if ahead:
                    if behind:
                        pool.wait_ge(exp_done, TT * number(u))
                    norms(after(u))
                if behind:
                    finish(before(u))
                if ahead > 1:
                    prepare(after(after(u)))

            run_units(pool, unit)
            finish((UNITS // 2 - 1, 1))

            pool.wait_ge(logit_done, UNITS)
            pool.wait_ge(x2_stored, 16 * UNITS)
            for n in range(2):
                pool.wait_ge(x2n_stored[n], 16 * UNITS // 2)
            nc.gpsimd.memset(x_got[:, :, :], 0.0).then_inc(got_clear, 1)
            nc.gpsimd.memset(o_got[:, :, :], 0.0).then_inc(got_clear, 1)
            pool.wait_ge(got_clear, 2)
            pool.wait_ge(idx_done, 2)

            def gather_x(e):
                for t in range(ST):
                    nc.gpsimd.indirect_dma_start(
                        x_got[:, t, :], None, x2n_dram,
                        bass.IndirectOffsetOnAxis(idx_all[:, e, t:t + 1], 0),
                        bounds_check=N_TOK - 1, oob_is_err=False).then_inc(x_gathered, 16)

            gather_x(0)
            for e in range(E):
                if e + 1 < E:
                    pool.wait_ge(xt_ready, ST * (e + 1))
                    gather_x(e + 1)
                if e > 0:
                    pool.wait_ge(scattered, 16 * ST * e)
                for t in range(ST):
                    nc.gpsimd.indirect_dma_start(
                        o_got[:, t, :], None, out_rows,
                        bass.IndirectOffsetOnAxis(idx_all[:, e, t:t + 1], 0),
                        bounds_check=N_TOK - 1, oob_is_err=False).then_inc(o_gathered, 16)
                for t in range(ST):
                    pool.wait_ge(y_done, ST * (e + 1) + t + 1)
                    nc.gpsimd.indirect_dma_start(
                        out_rows, bass.IndirectOffsetOnAxis(idx_all[:, e, t:t + 1], 0), o_got[:, t, :], None,
                        bounds_check=N_TOK - 1, oob_is_err=False).then_inc(scattered, 16)

        @block.scalar
        def _(act):
            def square_queries(u, reused):
                n = number(u)
                act.wait_ge(xt_done, n + 1)
                if reused:
                    act.wait_ge(ssq_done, n)
                nc.scalar.activation(x_sq[:, :], bank_m[:, :], ACT.Square).then_inc(xsq_done, 1)

            def take_v(u, behind):
                n = number(u)
                act.wait_ge(v_ready, n + 1)
                if behind > 1:
                    act.wait_ge(pv_done, TT * (n - 1))
                nc.scalar.activation(v_t[u[1]][:, :, 0:4:3, :],
                                     bank_t[:, :].rearrange("p (t h d) -> p t h d", t=TT, h=2),
                                     ACT.Copy).then_inc(v_taken, 1)
                if behind:
                    act.wait_ge(ssk_done, n)
                nc.scalar.activation(c_sq[:, :], bank_t[:, :], ACT.Square).then_inc(csq_done, 1)

            def exponentials(u, t, reused):
                g = TT * number(u) + t
                act.wait_ge(scores_ready, g + 1)
                if reused:
                    act.wait_ge(pv_done, g - 1)
                for h in range(2):
                    last = nc.scalar.activation(prob[h][t % 2][:, :], s_ps[:, 2 * (t % 2) + h, :], ACT.Exp,
                                                scale=rnorm[u[1]][:, 0, t, h:h + 1])
                last.then_inc(exp_done, 1)

            def take_o(u, reused):
                n = number(u)
                act.wait_ge(pv_done, TT * (n + 1))
                if reused:
                    act.wait_ge(on_done, n)
                nc.scalar.activation(p_sum[0:DH, :], o_ps[0][DH:P, :], ACT.Copy)
                nc.scalar.activation(p_sum[DH:P, :], o_ps[1][0:DH, :], ACT.Copy).then_inc(sum_taken, 1)
                nc.scalar.activation(o_sb[0:DH, :], o_ps[0][0:DH, :], ACT.Copy)
                nc.scalar.activation(o_sb[DH:P, :], o_ps[1][DH:P, :], ACT.Copy).then_inc(o_taken, 1)

            def take_x2t(u):
                act.wait_ge(x2t_ready, number(u) + 1)
                nc.scalar.activation(x2n_t[:, :, :], bank_t[:, :].rearrange("p (k t) -> p k t", k=KD),
                                     ACT.Copy).then_inc(x2t_taken, 1)

            act.wait_ge(v_ones, 2)
            square_queries((0, 0), False)
            take_v((0, 0), 0)
            act.wait_ge(rnorm_done, 1)

            def unit(u, behind, ahead):
                exponentials(u, 0, behind > 0)
                if ahead:
                    square_queries(after(u), True)
                    take_v(after(u), behind + 1)
                exponentials(u, 1, behind > 0)
                exponentials(u, 2, True)
                exponentials(u, 3, True)
                if behind:
                    take_x2t(before(u))
                take_o(u, behind > 0)
                if ahead:
                    act.wait_ge(rnorm_done, number(u) + 2)

            run_units(act, unit)
            take_x2t((UNITS // 2 - 1, 1))

            act.wait_ge(margin_done, 1)
            nc.scalar.activation(p_exp[:, :, :], margin[:, :, :], ACT.Exp, scale=-1.0).then_inc(e_neg, 1)

            def split_hi(e, c):
                act.wait_ge(raw_in[c % RAW_BUFS], 32 * ((CHUNKS // RAW_BUFS) * e + c // RAW_BUFS + 1))
                nc.scalar.activation(w_hi[c % SPLIT_BUFS][:, :], raw[c % RAW_BUFS][:, :], ACT.Copy
                                     ).then_inc(whi_done, 1)

            for c in range(AHEAD):
                split_hi(0, c)
            act.wait_ge(found_ready, E)

            def expert(e, last):
                for m in range(MT):
                    n = MT * e + m
                    act.wait_ge(z_ready, n + 1)
                    nc.scalar.activation(h_f[m % 2][:, :], z_ps[m % 2][:, :], ACT.Gelu)
                    nc.scalar.activation(h_hi[m % 2][:, :], z_ps[m % 2][:, :], ACT.Gelu).then_inc(gelu_done, 1)
                    if m % CHUNK_M == 0:
                        c = m // CHUNK_M + AHEAD
                        if c < CHUNKS:
                            split_hi(e, c)
                        elif not last:
                            split_hi(e + 1, c - CHUNKS)

            run_experts(act, expert)

        @block.vector
        def _(dve):
            def statistics(u):
                n = number(u)
                dve.wait_ge(x_in[u[1]], 16 * (u[0] + 1))
                nc.vector.bn_stats(stats[:, :], x_all[:, bass.ds(n, 1), :].rearrange("p a d -> p (a d)")
                                   ).then_inc(bn_done, 1)
                dve.wait_ge(bn_done, n + 1)
                nc.vector.memset(pad[:, :], 0.0)
                nc.vector.bn_aggr(mv[:, :], stats[:, :]).then_inc(mv_done, 1)
                dve.wait_ge(mv_done, n + 1)
                nc.vector.tensor_scalar(var_e[:, :], mv[:, 1:2], LN_EPS, None, ALU.add).then_inc(var_done, 1)

            def normalize(u):
                n = number(u)
                dve.wait_ge(rstd_done, n + 1)
                nc.vector.tensor_scalar(x_norm[:, :], x_all[:, bass.ds(n, 1), :].rearrange("p a d -> p (a d)"),
                                        mv[:, 0:1], rstd[:, 0:1], ALU.subtract, ALU.mult).then_inc(xn_done, 1)

            def split_keys(u, reused):
                n = number(u)
                dve.wait_ge(c_in[u[1]], 16 * (u[0] + 1))
                if reused:
                    dve.wait_ge(scores_ready, TT * (n - 1))
                nc.vector.tensor_copy(k_hi[u[1]][:, :], c_sb[u[1]][:, :]).then_inc(khi_done, 1)
                dve.wait_ge(khi_done, n + 1)
                nc.vector.tensor_tensor(k_lo[u[1]][:, :], c_sb[u[1]][:, :], k_hi[u[1]][:, :].bitcast(F32),
                                        ALU.subtract).then_inc(k_split, 1)

            def sum_squares(u):
                n = number(u)
                dve.wait_ge(xsq_done, n + 1)
                nc.vector.tensor_reduce(ss[:, 8:16], x_sq[:, :].rearrange("p (g d) -> p g d", d=DH), AX_X,
                                        ALU.add).then_inc(ssq_done, 1)
                dve.wait_ge(csq_done, n + 1)
                nc.vector.tensor_reduce(ss[:, 0:8], c_sq[:, :].rearrange("p (g d) -> p g d", d=DH), AX_X,
                                        ALU.add).then_inc(ssk_done, 1)
                dve.wait_ge(ssk_done, n + 1)
                nc.vector.tensor_scalar(ss_max[:, :], ss[:, :], NORM_EPS2, None, ALU.max).then_inc(ss_done, 1)

            def take_logits(u):
                n = number(u)
                dve.wait_ge(logit_ready, n + 1)
                nc.vector.tensor_tensor(logits[:, bass.ds(n, 1), :].rearrange("p a e -> p (a e)"),
                                        bank_t[:, 0:E], bgb[:, :], ALU.add).then_inc(logit_done, 1)

            def queries(u, follow):
                n = number(u)
                dve.wait_ge(rq_ready, n + 1)
                nc.vector.scalar_tensor_tensor(q_f[:, :], x_norm[:, :], ALPHA, bank_m[:, :], ALU.mult, ALU.mult
                                               ).then_inc(q_done, 1)
                dve.wait_ge(q_done, n + 1)
                nc.vector.tensor_copy(q_hi[u[1]][:, :], q_f[:, :]).then_inc(qhi_done, 1)
                if follow is not None:
                    normalize(follow)
                dve.wait_ge(qhi_done, n + 1)
                nc.vector.tensor_tensor(q_lo[u[1]][:, :], q_f[:, :], q_hi[u[1]][:, :].bitcast(F32),
                                        ALU.subtract).then_inc(q_split, 1)

            def widen_queries(u):
                dve.wait_ge(rnorm_done, number(u) + 1)
                nc.vector.tensor_copy(wide_q[:, :, :, :], rnorm[u[1]][:, 1, :, :].unsqueeze(3)
                                      .broadcast_to([P, TT, 2, DH])).then_inc(wq_done, 1)

            def invert_sums(u):
                n = number(u)
                dve.wait_ge(sum_taken, n + 1)
                nc.vector.reciprocal(p_inv[:, :], p_sum[:, :]).then_inc(inv_done, 1)

            def residual(u):
                n = number(u)
                xu = x_all[:, bass.ds(n, 1), :].rearrange("p a d -> p (a d)")
                dve.wait_ge(o_taken, n + 1)
                dve.wait_ge(inv_done, n + 1)
                nc.vector.tensor_tensor(o_norm[:, :], o_sb[:, :], p_inv[:, :], ALU.mult).then_inc(on_done, 1)
                dve.wait_ge(on_done, n + 1)
                nc.vector.tensor_tensor(xu, xu, o_norm[:, :], ALU.add).then_inc(x2_done, 1)
                dve.wait_ge(x2_done, n + 1)
                nc.vector.memset(pad[:, :], 0.0)
                nc.vector.bn_stats(stats2[:, :], xu).then_inc(bn2_done, 1)
                dve.wait_ge(bn2_done, n + 1)
                nc.vector.memset(pad2[:, :], 0.0)
                nc.vector.bn_aggr(mv2[:, :], stats2[:, :]).then_inc(mv2_done, 1)
                dve.wait_ge(mv2_done, n + 1)
                nc.vector.tensor_scalar(var2_e[:, :], mv2[:, 1:2], LN_EPS, None, ALU.add).then_inc(var2_done, 1)

            def normalize_x2(u, reused):
                n = number(u)
                xu = x_all[:, bass.ds(n, 1), :].rearrange("p a d -> p (a d)")
                dve.wait_ge(rstd2_done, n + 1)
                if reused:
                    dve.wait_ge(x2n_stored[u[1]], 16 * u[0])
                nc.vector.tensor_scalar(x2n[u[1]][:, :], xu, mv2[:, 0:1], rstd2[:, 0:1], ALU.subtract, ALU.mult
                                        ).then_inc(x2n_done, 1)

            dve.wait_ge(cst_in, 16)
            dve.wait_ge(bg_in, 16)
            dve.wait_ge(wg_in, 16)
            nc.vector.tensor_copy(wg[:, :, :].rearrange("p k (r e) -> p k r e", e=E),
                                  wg_e[:, :, :].unsqueeze(2).broadcast_to([P, KD, NARROW // E, E])
                                  ).then_inc(wg_done, 1)
            statistics((0, 0))
            normalize((0, 0))
            split_keys((0, 0), False)
            statistics((0, 1))
            sum_squares((0, 0))
            widen_queries((0, 0))
            queries((0, 0), (0, 1))
            split_keys((0, 1), False)

            def unit(u, behind, ahead):
                if behind:
                    invert_sums(before(u))
                if ahead:
                    sum_squares(after(u))
                if behind:
                    residual(before(u))
                if ahead > 1:
                    statistics(after(after(u)))
                if ahead:
                    widen_queries(after(u))
                if behind:
                    normalize_x2(before(u), behind > 2)
                if ahead > 1:
                    split_keys(after(after(u)), True)
                if ahead:
                    queries(after(u), after(after(u)) if ahead > 1 else None)
                if behind:
                    take_logits(before(u))

            run_units(dve, unit)
            end = (UNITS // 2 - 1, 1)
            invert_sums(end)
            residual(end)
            normalize_x2(end, True)
            take_logits(end)

            done = [0]

            def link(ins):
                done[0] += 1
                ins.then_inc(step, 1)
                dve.wait_ge(step, done[0])

            dve.wait_ge(logit_done, UNITS)
            four_d = [P, UNITS, E, E]
            l_j = logits[:, :, :].unsqueeze(2).broadcast_to(four_d)
            l_i = logits[:, :, :].unsqueeze(3).broadcast_to(four_d)
            tie = cst[:, C_TIE:C_TIE + E * E].rearrange("p (i j) -> p i j", i=E).unsqueeze(1).broadcast_to(four_d)
            offd = cst[:, C_OFFD:C_OFFD + E * E].rearrange("p (i j) -> p i j", i=E).unsqueeze(1).broadcast_to(four_d)
            link(nc.vector.tensor_tensor(cmp_a[:, :, :, :], l_j, l_i, ALU.is_gt))
            link(nc.vector.tensor_tensor(cmp_b[:, :, :, :], l_j, l_i, ALU.is_equal))
            link(nc.vector.tensor_tensor(cmp_b[:, :, :, :], cmp_b[:, :, :, :], tie, ALU.mult))
            link(nc.vector.tensor_tensor(cmp_a[:, :, :, :], cmp_a[:, :, :, :], cmp_b[:, :, :, :], ALU.add))
            link(nc.vector.tensor_reduce(rank[:, :, :], cmp_a[:, :, :, :], AX_X, ALU.add))
            link(nc.vector.tensor_scalar(assigned[:, :, :], rank[:, :, :], 1.5, None, ALU.is_lt))
            link(nc.vector.tensor_tensor(al[:, :, :], assigned[:, :, :], logits[:, :, :], ALU.mult))
            link(nc.vector.tensor_tensor(cmp_b[:, :, :, :], al[:, :, :].unsqueeze(2).broadcast_to(four_d), offd,
                                         ALU.mult))
            link(nc.vector.tensor_reduce(rank[:, :, :], cmp_b[:, :, :, :], AX_X, ALU.add))
            nc.vector.tensor_tensor(margin[:, :, :], logits[:, :, :], rank[:, :, :], ALU.subtract
                                    ).then_inc(margin_done, 1)
            dve.wait_ge(margin_done, 1)
            link(nc.vector.tensor_scalar(key[:, :, :], margin[:, :, :], KEY_CLAMP, -KEY_CLAMP, ALU.min, ALU.max))
            link(nc.vector.tensor_scalar(key_b[:, :, :], assigned[:, :, :], -KEY_OUT, KEY_OUT, ALU.mult, ALU.add))
            link(nc.vector.tensor_tensor(key[:, :, :], key[:, :, :], assigned[:, :, :], ALU.mult))
            link(nc.vector.tensor_tensor(key[:, :, :], key[:, :, :], key_b[:, :, :], ALU.add))
            nc.vector.tensor_copy(key_w[:, :, :, :], key[:, :, :].unsqueeze(3).broadcast_to([P, UNITS, E, WAYS])
                                  ).then_inc(key_done, 1)
            link(nc.vector.memset(low[:, :], KEY_LO))
            dve.wait_ge(e_neg, 1)
            link(nc.vector.tensor_scalar(p_exp[:, :, :], p_exp[:, :, :], 1.0, None, ALU.add))
            link(nc.vector.reciprocal(p_sel[:, :, :], p_exp[:, :, :]))

            dve.wait_ge(key_t, 1)
            dve.wait_ge(key_done, 1)
            width = KEY_RANGE / WAYS
            for r in range(ROUNDS):
                link(nc.vector.tensor_scalar(thr[:, :], cst[:, C_KVEC:C_KVEC + 1], width, low[:, 0:1],
                                             ALU.mult, ALU.add))
                link(nc.vector.tensor_scalar(junk[:, :].rearrange("p (a t) -> p a t", a=4), four[:, :, :],
                                             thr[:, 0:1], None, ALU.is_ge, ALU.add, accum_out=count[:, :]))
                nc.vector.tensor_scalar(enough[:, :], count[:, :], CAP - 0.5, None, ALU.is_ge
                                        ).then_inc(enough_done, 1)
                dve.wait_ge(n_ready, r + 1)
                link(nc.vector.scalar_tensor_tensor(low[:, :], bank_m[:, 0:1], width, low[:, :],
                                                    ALU.mult, ALU.add))
                if r < ROUNDS - 1:
                    width /= WAYS
            nc.vector.tensor_scalar(lowpick[:, :], cst[:, C_PICK:C_PICK + E], low[:, 0:1], None, ALU.mult
                                    ).then_inc(pick_done, 1)
            dve.wait_ge(t_ready, 1)
            link(nc.vector.tensor_copy(t_low[:, :], bank_t[:, 0:E]))
            link(nc.vector.tensor_scalar(t_high[:, :], t_low[:, :], width, None, ALU.add))

            three_d = [P, E, UNITS]
            key_e = key[:, :, :].rearrange("p t e -> p e t")
            link(nc.vector.tensor_tensor(ge[:, :, :], key_e, t_low[:, :].unsqueeze(2).broadcast_to(three_d),
                                         ALU.is_ge))
            link(nc.vector.tensor_tensor(mask[:, :, 0, :], key_e, t_high[:, :].unsqueeze(2).broadcast_to(three_d),
                                         ALU.is_ge))
            nc.vector.tensor_tensor(mask[:, :, 1, :], ge[:, :, :], mask[:, :, 0, :], ALU.subtract
                                    ).then_inc(mask_done, 1)
            dve.wait_ge(pre_ready, 1)
            flat = E * 2 * UNITS
            pre_flat = pre[:, :, :, :].rearrange("p e g t -> p (e g t)")
            link(nc.vector.tensor_copy(tot[:, :], two[0][:, flat:2 * flat]))
            link(nc.vector.tensor_tensor_scan(scan[:, :], cst[:, C_RESET:C_RESET + flat], tot[:, :], 0.0,
                                              ALU.mult, ALU.add))
            link(nc.vector.tensor_tensor(pre_flat, two[0][:, 0:flat], scan[:, :], ALU.add))
            link(nc.vector.tensor_tensor(pre_flat, pre_flat, tot[:, :], ALU.subtract))
            above = scan[:, :].rearrange("p (e g t) -> p e g t", e=E, g=2)[:, :, 0, UNITS - 1:UNITS]
            link(nc.vector.tensor_tensor(pre[:, :, 1, :], pre[:, :, 1, :], above.broadcast_to(three_d), ALU.add))
            link(nc.vector.tensor_tensor(slot[:, :, :], mask[:, :, 0, :], pre[:, :, 0, :], ALU.mult))
            link(nc.vector.tensor_tensor(slot_b[:, :, :], mask[:, :, 1, :], pre[:, :, 1, :], ALU.mult))
            link(nc.vector.tensor_tensor(slot[:, :, :], slot[:, :, :], slot_b[:, :, :], ALU.add))
            link(nc.vector.tensor_scalar(s_c[:, :, :], ge[:, :, :], -NO_SLOT, NO_SLOT, ALU.mult, ALU.add))
            link(nc.vector.tensor_tensor(slot[:, :, :], slot[:, :, :], s_c[:, :, :], ALU.add))
            link(nc.vector.tensor_scalar(s_hi[:, :, :], slot[:, :, :], float(P), None, ALU.is_ge))
            for s in range(2, ST):
                link(nc.vector.scalar_tensor_tensor(s_hi[:, :, :], slot[:, :, :], float(s * P), s_hi[:, :, :],
                                                    ALU.is_ge, ALU.add))
            link(nc.vector.scalar_tensor_tensor(s_lo[:, :, :], s_hi[:, :, :], -float(P), slot[:, :, :],
                                                ALU.mult, ALU.add))
            tok = cst[:, C_TOK:C_TOK + UNITS].unsqueeze(1).broadcast_to(three_d)
            for s in range(ST):
                link(nc.vector.scalar_tensor_tensor(pay[:, :, :, s, 0], s_hi[:, :, :], float(s), tok,
                                                    ALU.is_equal, ALU.mult))
                link(nc.vector.scalar_tensor_tensor(pay[:, :, :, s, 1], s_hi[:, :, :], float(s),
                                                    p_sel[:, :, :].rearrange("p t e -> p e t"),
                                                    ALU.is_equal, ALU.mult))
            dve.wait_ge(x2_stored, 16 * UNITS)
            for n in range(2):
                dve.wait_ge(x2n_stored[n], 16 * UNITS // 2)
            oh_d = [P, UNITS, P]
            for e in range(E):
                if e >= 2:
                    dve.wait_ge(found_ready, e - 1)
                nc.vector.tensor_tensor(onehot[e % 2][:, :, :],
                                        cst[:, C_IOTA:C_IOTA + P].unsqueeze(1).broadcast_to(oh_d),
                                        s_lo[:, e, :].unsqueeze(2).broadcast_to(oh_d), ALU.is_equal
                                        ).then_inc(oh_done, 1)
            dve.wait_ge(found_ready, E)
            link(nc.vector.tensor_copy(found[:, :, :, :].rearrange("p e s c -> p (e s c)"),
                                       two[1][:, 0:E * ST * 2]))
            link(nc.vector.tensor_scalar(f_empty[:, :, :], found[:, :, :, 0], 0.0, 2.0 * N_TOK,
                                         ALU.is_equal, ALU.mult))
            nc.vector.tensor_copy(prob_all[:, :, :], found[:, :, :, 1]).then_inc(idx_done, 1)
            link(nc.vector.tensor_tensor(f_idx[:, :, :], found[:, :, :, 0], f_empty[:, :, :], ALU.add))
            nc.vector.tensor_scalar(idx_all[:, :, :], f_idx[:, :, :], -1.0, None, ALU.add).then_inc(idx_done, 1)

            nc.vector.memset(credit[:, :], 0.0).then_inc(y_done, ST)

            def split_lo(e, c):
                n = CHUNKS * e + c
                dve.wait_ge(whi_done, n + 1)
                nc.vector.tensor_tensor(w_lo[c % SPLIT_BUFS][:, :], raw[c % RAW_BUFS][:, :],
                                        w_hi[c % SPLIT_BUFS][:, :].bitcast(F32), ALU.subtract
                                        ).then_inc(wlo_done, 1)

            def split_tokens(e, t, parity):
                g = ST * e + t
                bank = (bank_t, bank_m)[t % 2][:, :].rearrange("p (a k t) -> p a k t", a=1, k=KD)
                hi = xt_hi[:, bass.ds(parity, 1), :, t * P:(t + 1) * P]
                lo = xt_lo[:, bass.ds(parity, 1), :, t * P:(t + 1) * P]
                dve.wait_ge(xt_ready, g + 1)
                nc.vector.tensor_copy(hi, bank).then_inc(xthi_done, 1)
                dve.wait_ge(xthi_done, g + 1)
                nc.vector.tensor_tensor(lo, bank, hi.bitcast(F32), ALU.subtract).then_inc(xt_split, 1)

            split_lo(0, 0)
            for t in range(ST):
                split_tokens(0, t, 0)
            for c in range(1, AHEAD):
                split_lo(0, c)

            def expert(e, last):
                for m in range(MT):
                    dve.wait_ge(gelu_done, MT * e + m + 1)
                    nc.vector.tensor_tensor(h_lo[m % 2][:, :], h_f[m % 2][:, :], h_hi[m % 2][:, :].bitcast(F32),
                                            ALU.subtract).then_inc(h_split, 1)
                    if m % CHUNK_M == 0:
                        c = m // CHUNK_M + AHEAD
                        if c < CHUNKS:
                            split_lo(e, c)
                        elif not last:
                            split_lo(e + 1, c - CHUNKS)
                    if not last and XT_AT <= m < XT_AT + ST:
                        split_tokens(e + 1, m - XT_AT, (e + 1) % 2)
                dve.wait_ge(o_gathered, 16 * ST * (e + 1))
                for t in range(ST):
                    dve.wait_ge(acc_ready, ST * e + t + 1)
                    nc.vector.scalar_tensor_tensor(o_got[:, t, :], acc_ps[:, t, :], prob_all[:, bass.ds(e, 1), t],
                                                   o_got[:, t, :], ALU.mult, ALU.add).then_inc(y_done, 1)

            run_experts(dve, expert)

        @block.tensor
        def _(pe):
            def transpose_queries(u):
                pe.wait_ge(xn_done, number(u) + 1)
                for t in range(TT):
                    last = nc.tensor.transpose(bank_m[:, t * P:(t + 1) * P], x_norm[:, t * P:(t + 1) * P], ident)
                last.then_inc(xt_done, 1)

            def values(u):
                pe.wait_ge(k_split, number(u) + 1)
                for t in range(TT):
                    last = nc.tensor.transpose(bank_t[:, t * P:(t + 1) * P], c_sb[u[1]][:, t * P:(t + 1) * P],
                                               ident)
                last.then_inc(v_ready, 1)

            def spread_queries(u):
                pe.wait_ge(wq_done, number(u) + 1)
                for t in range(TT):
                    last = nc.tensor.transpose(bank_m[:, t * P:(t + 1) * P],
                                               wide_q[:, t, :, :].rearrange("p h d -> p (h d)"), ident)
                last.then_inc(rq_ready, 1)

            def scores(u, t, reused):
                if reused:
                    pe.wait_ge(exp_done, TT * number(u) + t - 1)
                for term, (k, q) in enumerate(((k_hi, q_hi), (k_hi, q_lo), (k_lo, q_hi))):
                    for h in range(2):
                        ch = slice(DH * h, DH * (h + 1))
                        last = nc.tensor.matmul(s_ps[:, 2 * (t % 2) + h, :], k[u[1]][ch, t * P:(t + 1) * P],
                                                q[u[1]][ch, :], start=(term == 0), stop=(term == 2))
                last.then_inc(scores_ready, 1)

            def weighted_values(u, t):
                pe.wait_ge(exp_done, TT * number(u) + t + 1)
                for h in range(2):
                    last = nc.tensor.matmul(o_ps[h][:, :], v_t[u[1]][:, t, 2 * h:2 * h + 2, :]
                                            .rearrange("p a d -> p (a d)"), prob[h][t % 2][:, :],
                                            start=(t == 0), stop=(t == TT - 1))
                last.then_inc(pv_done, 1)

            def transpose_x2(u):
                pe.wait_ge(x2n_done, number(u) + 1)
                for k in range(KD):
                    last = nc.tensor.transpose(bank_t[:, k * P:(k + 1) * P], x2n[u[1]][:, k * P:(k + 1) * P],
                                               ident)
                last.then_inc(x2t_ready, 1)

            def router_logits(u):
                pe.wait_ge(x2t_taken, number(u) + 1)
                for k in range(KD):
                    last = nc.tensor.matmul(bank_t[:, 0:NARROW], x2n_t[:, k, :], wg[:, k, :],
                                            start=(k == 0), stop=(k == KD - 1))
                last.then_inc(logit_ready, 1)

            pe.wait_ge(cst_in, 16)
            pe.wait_ge(wg_done, 1)
            transpose_queries((0, 0))
            values((0, 0))
            spread_queries((0, 0))
            pe.wait_ge(q_split, 1)
            scores((0, 0), 0, False)

            def unit(u, behind, ahead):
                n = number(u)
                scores(u, 1, behind > 0)
                if ahead:
                    pe.wait_ge(q_done, n + 1)
                    transpose_queries(after(u))
                    if behind > 1:
                        pe.wait_ge(logit_done, n - 1)
                    else:
                        pe.wait_ge(csq_done, n + 1)
                    values(after(u))
                if behind:
                    pe.wait_ge(o_taken, n)
                else:
                    pe.wait_ge(v_taken, 1)
                weighted_values(u, 0)
                scores(u, 2, True)
                weighted_values(u, 1)
                scores(u, 3, True)
                weighted_values(u, 2)
                if ahead:
                    spread_queries(after(u))
                if behind:
                    pe.wait_ge(csq_done, n + (2 if ahead else 1))
                    transpose_x2(before(u))
                weighted_values(u, 3)
                if behind:
                    router_logits(before(u))
                if ahead:
                    pe.wait_ge(q_split, n + 2)
                    scores(after(u), 0, True)

            run_units(pe, unit)
            end = (UNITS // 2 - 1, 1)
            pe.wait_ge(logit_done, UNITS - 1)
            transpose_x2(end)
            router_logits(end)

            pe.wait_ge(key_done, 1)
            for t in range(UNITS):
                last = nc.tensor.transpose(four[:, t // 4, (t % 4) * P:(t % 4 + 1) * P],
                                           key_w[:, t, :, :].rearrange("p e w -> p (e w)"), ident)
            last.then_inc(key_t, 1)
            for r in range(ROUNDS):
                pe.wait_ge(enough_done, r + 1)
                nc.tensor.matmul(bank_m[:, 0:1], cst[:, C_BLOCK:C_BLOCK + P], enough[:, :], start=True, stop=True
                                 ).then_inc(n_ready, 1)
            pe.wait_ge(pick_done, 1)
            nc.tensor.matmul(bank_t[:, 0:E], cst[:, C_ONES:C_ONES + P], lowpick[:, :], start=True, stop=True
                             ).then_inc(t_ready, 1)
            pe.wait_ge(mask_done, 1)
            flat = E * 2 * UNITS
            mask_flat = mask[:, :, :, :].rearrange("p e g t -> p (e g t)")
            nc.tensor.matmul(two[0][:, 0:flat], cst[:, C_TRI:C_TRI + P], mask_flat, start=True, stop=True)
            nc.tensor.matmul(two[0][:, flat:2 * flat], cst[:, C_ONES:C_ONES + P], mask_flat, start=True,
                             stop=True).then_inc(pre_ready, 1)
            for e in range(E):
                pe.wait_ge(oh_done, e + 1)
                for t in range(UNITS):
                    last = nc.tensor.matmul(two[1][:, e * ST * 2:(e + 1) * ST * 2], onehot[e % 2][:, t, :],
                                            pay[:, e, t, :, :].rearrange("p s c -> p (s c)"),
                                            start=(t == 0), stop=(t == UNITS - 1))
                last.then_inc(found_ready, 1)

            def transpose_tokens(t):
                bank = (bank_t, bank_m)[t % 2]
                for k in range(KD):
                    last = nc.tensor.transpose(bank[:, k * P:(k + 1) * P], x_got[:, t, k * P:(k + 1) * P], ident)
                last.then_inc(xt_ready, 1)

            def up(e, m, parity):
                pe.wait_ge(wlo_done, CHUNKS * e + m // CHUNK_M + 1)
                c, z = (m // CHUNK_M) % SPLIT_BUFS, z_ps[m % 2]
                for k in range(KD):
                    w = slice(k * CW + (m % CHUNK_M) * P, k * CW + (m % CHUNK_M + 1) * P)
                    x_h = xt_hi[:, bass.ds(parity, 1), k, :].rearrange("p a t -> p (a t)")
                    x_l = xt_lo[:, bass.ds(parity, 1), k, :].rearrange("p a t -> p (a t)")
                    nc.tensor.matmul(z[:, :], w_hi[c][:, w], x_h, start=(k == 0), stop=False)
                    nc.tensor.matmul(z[:, :], w_hi[c][:, w], x_l, start=False, stop=False)
                    last = nc.tensor.matmul(z[:, :], w_lo[c][:, w], x_h, start=False, stop=(k == KD - 1))
                last.then_inc(z_ready, 1)

            def down(e, m):
                c = (m // CHUNK_M) % SPLIT_BUFS
                w = slice(HALF + (m % CHUNK_M) * D, HALF + (m % CHUNK_M + 1) * D)
                pe.wait_ge(h_split, MT * e + m + 1)
                for t in range(ST):
                    if m == 0:
                        pe.wait_ge(y_done, ST * e + t + 1)
                    h = slice(t * P, (t + 1) * P)
                    nc.tensor.matmul(acc_ps[:, t, :], h_hi[m % 2][:, h], w_hi[c][:, w],
                                     start=(m == 0), stop=False)
                    nc.tensor.matmul(acc_ps[:, t, :], h_hi[m % 2][:, h], w_lo[c][:, w], start=False, stop=False)
                    last = nc.tensor.matmul(acc_ps[:, t, :], h_lo[m % 2][:, h], w_hi[c][:, w], start=False,
                                            stop=(m == MT - 1))
                    if m == MT - 1:
                        last.then_inc(acc_ready, 1)

            pe.wait_ge(x_gathered, 16 * ST)
            for t in range(ST):
                if t >= 2:
                    pe.wait_ge(xt_split, t - 1)
                transpose_tokens(t)
            pe.wait_ge(xt_split, ST)
            up(0, 0, 0)

            def expert(e, last):
                for m in range(MT):
                    if m < MT - 1:
                        up(e, m + 1, e % 2)
                    elif not last:
                        pe.wait_ge(xt_split, ST * (e + 2))
                        up(e + 1, 0, (e + 1) % 2)
                    down(e, m)
                    if not last and XT_AT <= m < XT_AT + ST:
                        if m == XT_AT:
                            pe.wait_ge(x_gathered, 16 * ST * (e + 2))
                        pe.wait_ge(xt_split, ST * (e + 1) + m - XT_AT - 1)
                        transpose_tokens(m - XT_AT)

            run_experts(pe, expert)


_INS = ["x", "ctx_2048", "L0_ffn_Wg", "L0_ffn_bg", "L0_ffn_W1", "L0_ffn_W2"]


def kernel(**inputs):
    import concourse.bacc as bacc
    import numpy as np
    from concourse.bass_utils import run_bass_kernel_spmd

    nc = bacc.Bacc("TRN2", target_bir_lowering=False, num_devices=1)
    arrays, args = {}, []
    for name, a in [(n, np.ascontiguousarray(inputs[n])) for n in _INS] + [("consts", constants())]:
        arrays[f"in_{name}"] = a
        args.append(nc.dram_tensor(f"in_{name}", a.shape, F32, kind="ExternalInput").ap())
    out = nc.dram_tensor("out_0", (B, S, D), F32, kind="ExternalOutput").ap()
    xattn_moe_kernel(nc, *args, out)
    r = run_bass_kernel_spmd(nc, [arrays], core_ids=[0])
    return r.results[0]["out_0"]
```

```python
from contextlib import ExitStack

import concourse.bass as bass
from concourse import mybir

F32 = mybir.dt.float32
F32R = mybir.dt.float32r
BF16 = mybir.dt.bfloat16
U32 = mybir.dt.uint32
ALU = mybir.AluOpType
ACT = mybir.ActivationFunctionType
AX_X = mybir.AxisListType.X

P = 128
B, S, D = 4, 512, 512
HEADS = 8
DH = S // HEADS
ALPHA = 5.0
NORM_EPS2 = 1e-24
LN_EPS = 1e-5
N_TOK = B * S
UNITS = N_TOK // P
TT = D // P
E, H = 4, 2048
CAP = N_TOK // E
ST = CAP // P
KD = D // P
MT = H // P
CHUNK_M = 2
CHUNKS = MT // CHUNK_M
RAW_BUFS, SPLIT_BUFS = 2, 4
AHEAD = 2
XT_AT = 8
CW = CHUNK_M * P
HALF = KD * CW

KEY_LO, KEY_RANGE, WAYS, ROUNDS = -32.0, 64.0, 32, 6
KEY_MAX, KEY_MIN, KEY_BEND, KEY_SQUEEZE = 16.64, -87.3, 15.0, 8.0
KEY_OUT = -128.0
NO_SLOT = 4096.0
SIGNS = 2 * CAP
QUARTERS = 4
PAY = 5
NO_TOKEN = 2.0 * N_TOK
EARLY = UNITS - 2

C_IDENT, C_BEFORE, C_ONES, C_BLOCK, C_IOTA = (P * n for n in range(5))
C_KVEC = 5 * P
C_PICK = C_KVEC + 1
C_TOK = C_PICK + E
C_TIE = C_TOK + 2 * UNITS
C_OFFD = C_TIE + E * E
C_RESET = C_OFFD + E * E
C_ALL = C_RESET + E * 2 * UNITS


def constants():
    import numpy as np

    c = np.zeros((P, C_ALL), np.float32)
    p = np.arange(P)
    c[:, C_IDENT:C_IDENT + P] = np.eye(P)
    c[:, C_BEFORE:C_BEFORE + P] = (p[:, None] < p[None, :]) - 1.0
    c[:, C_ONES:C_ONES + P] = 1
    c[:, C_BLOCK:C_BLOCK + P] = p[:, None] // WAYS == p[None, :] // WAYS
    c[:, C_IOTA:C_IOTA + P] = p[None, :]
    c[:, C_KVEC] = p % WAYS + 1
    c[:, C_PICK:C_PICK + E] = p[:, None] == WAYS * np.arange(E)[None, :]
    c[:, C_TOK:C_TOK + UNITS] = P * np.arange(UNITS)[None, :] - NO_TOKEN
    c[:, C_TOK + UNITS:C_TIE] = p[:, None]
    i, j = np.divmod(np.arange(E * E), E)
    c[:, C_TIE:C_TIE + E * E] = j < i
    c[:, C_OFFD:C_OFFD + E * E] = j != i
    c[:, C_RESET:C_ALL] = np.arange(E * 2 * UNITS) % (2 * UNITS) != 0
    return c


def xattn_moe_kernel(nc, x, ctx_in, Wg, bg, W1, W2, consts, out):
    x_rows = x.rearrange("b s d -> (b s) d")
    c_rows = ctx_in.rearrange("b s d -> (b s) d")
    out_rows = out.rearrange("b s d -> (b s) d")
    x2n_dram = nc.dram_tensor("x2n_dram", (N_TOK, D), F32, kind="Internal").ap()

    with ExitStack() as stack:
        def sem(name):
            return stack.enter_context(nc.semaphore(name))

        def keep(name, shape, dt=F32):
            return stack.enter_context(nc.sbuf_tensor(name, shape, dt))

        cst = keep("cst", [P, C_ALL])
        wg = keep("wg", [P, KD, E])
        bgb = keep("bgb", [P, E])
        raw = [keep(f"raw{n}", [P, 2 * HALF]) for n in range(RAW_BUFS)]
        w_hi = [keep(f"w_hi{n}", [P, 2 * HALF], F32R) for n in range(SPLIT_BUFS)]
        w_lo = [keep(f"w_lo{n}", [P, 2 * HALF], F32R) for n in range(SPLIT_BUFS)]
        logits = keep("logits", [P, UNITS, E])
        cmp_a = keep("cmp_a", [P, UNITS, E, E])
        cmp_b = keep("cmp_b", [P, UNITS, E, E])
        rank = keep("rank", [P, UNITS, E])
        al = keep("al", [P, UNITS, E])
        margin = keep("margin", [P, UNITS, E])
        p_exp = keep("p_exp", [P, UNITS, E])
        p_sel = keep("p_sel", [P, UNITS, E])
        key = keep("key", [P, UNITS, E])
        key_b = keep("key_b", [P, UNITS, E])
        other = keep("other", [P, UNITS, E])
        clamped = keep("clamped", [P, UNITS, E])
        squeezed = keep("squeezed", [P, UNITS, E])
        bent = keep("bent", [P, UNITS, E])
        key_w = keep("key_w", [P, UNITS, E, WAYS])
        thr = keep("thr", [P, 1])
        low = keep("low", [P, 1])
        count = keep("count", [P, 1])
        enough = keep("enough", [P, 1], BF16)
        junk = keep("junk", [P, N_TOK - SIGNS], BF16)
        junk_a = keep("junk_a", [P, SIGNS], BF16)
        excess = keep("excess", [P, 1])
        rest0 = keep("rest0", [P, 1])
        n_next = keep("n_next", [P, 1])
        low_new = keep("low_new", [P, 1])
        high = keep("high", [P, 1])
        lowpick = keep("lowpick", [P, 2, E])
        t_low = keep("t_low", [P, E])
        t_high = keep("t_high", [P, E])
        mask = keep("mask", [P, E, 2, UNITS], BF16)
        before_b = keep("before_b", [P, P], BF16)
        ones_b = keep("ones_b", [P, P], BF16)
        block_b = keep("block_b", [P, P], BF16)
        thr_base = keep("thr_base", [P, 1])
        count0 = keep("count0", [P, 1])
        p_rest = keep("p_rest", [P, UNITS, E])
        parts = keep("parts", [P, E, UNITS, PAY], BF16)
        sel = keep("sel", [P, E, UNITS, ST], BF16)
        ge = keep("ge", [P, E, UNITS])
        scan = keep("scan", [P, E * 2 * UNITS])
        pre = keep("pre", [P, E, 2, UNITS])
        slot = keep("slot", [P, E, UNITS])
        s_hi = keep("s_hi", [P, E, UNITS])
        s_c = keep("s_c", [P, E, UNITS])
        s_lo = keep("s_lo", [P, E, UNITS])
        pay = keep("pay", [P, E, UNITS, ST, PAY], BF16)
        row = keep("row", [P, E, ST])
        idx_all = keep("idx_all", [P, E, ST], U32)
        prob_all = keep("prob_all", [P, E, ST])
        credit = keep("credit", [P, 1])
        ident = cst[:, C_IDENT:C_IDENT + P]

        with ExitStack() as phase:
            def att(name, shape, dt=F32):
                return phase.enter_context(nc.sbuf_tensor(name, shape, dt))

            x_all = att("x_all", [P, UNITS, D])
            c_sb = [att(f"c_sb{n}", [P, D]) for n in range(2)]
            c_sq = att("c_sq", [P, D])
            x_norm = att("x_norm", [P, D])
            x_sq = att("x_sq", [P, D])
            k_hl = [[att(f"k_hl{h}{n}", [P, D], F32R) for n in range(2)] for h in range(2)]
            q_f = att("q_f", [P, D])
            q_hh = [[att(f"q_hh{h}{n}", [P, D], F32R) for n in range(2)] for h in range(2)]
            q_lo = [att(f"q_lo{n}", [P, D], F32R) for n in range(2)]
            v_t = [att(f"v_t{n}", [P, TT, 4, DH]) for n in range(2)]
            prob = [[att(f"prob{h}{n}", [P, D]) for n in range(2)] for h in range(2)]
            o_sb = att("o_sb", [P, D])
            p_sum = att("p_sum", [P, D])
            p_inv = att("p_inv", [P, D])
            o_norm = att("o_norm", [P, D])
            x2n = [att(f"x2n{n}", [P, D]) for n in range(2)]
            x2n_t = att("x2n_t", [P, KD, P])
            stats = att("stats", [P, 6])
            mv = att("mv", [P, 2])
            var_e = att("var_e", [P, 1])
            rstd = att("rstd", [P, 1])
            pad = att("pad", [P, 1])
            pad2 = att("pad2", [P, 1])
            stats2 = att("stats2", [P, 6])
            mv2 = att("mv2", [P, 2])
            var2_e = att("var2_e", [P, 1])
            rstd2 = att("rstd2", [P, 1])
            ss = att("ss", [P, 16])
            ss_max = att("ss_max", [P, 16])
            rnorm = [att(f"rnorm{n}", [P, 2, TT, 2]) for n in range(2)]
            wide_q = att("wide_q", [P, TT, 2, DH])
            power = att("power", [P, 16])

        with ExitStack() as phase:
            def ffn(name, shape, dt=F32):
                return phase.enter_context(nc.sbuf_tensor(name, shape, dt))

            xt_hi = ffn("xt_hi", [P, 2, KD, CAP], F32R)
            xt_lo = ffn("xt_lo", [P, 2, KD, CAP], F32R)
            x_got = ffn("x_got", [P, ST, D])
            o_got = ffn("o_got", [P, ST, D])
            h_f = [ffn(f"h_f{n}", [P, CAP]) for n in range(2)]
            h_hi = [ffn(f"h_hi{n}", [P, CAP], F32R) for n in range(2)]
            h_lo = [ffn(f"h_lo{n}", [P, CAP], F32R) for n in range(2)]
            onehot = [ffn(f"onehot{n}", [P, UNITS, P], BF16) for n in range(2)]

        four = stack.enter_context(nc.psum_tensor("four", [P, 4, 512], F32))
        two = [stack.enter_context(nc.psum_tensor(f"two{n}", [P, 512], F32)) for n in range(2)]
        bank_t = stack.enter_context(nc.psum_tensor("bank_t", [P, 512], F32))
        bank_m = stack.enter_context(nc.psum_tensor("bank_m", [P, 512], F32))
        s_ps, o_ps = four, two
        four_flat = four[:, :, :].rearrange("p a t -> p (a t)")
        acc_ps, z_ps = four, two

        ident_in = sem("ident_in")
        cst_in = sem("cst_in")
        wg_in = sem("wg_in")
        bg_in = sem("bg_in")
        bf_done = sem("bf_done")
        x_in = [sem(f"x_in{n}") for n in range(2)]
        c_in = [sem(f"c_in{n}") for n in range(2)]
        v_ones = sem("v_ones")
        power_set = sem("power_set")
        bn_done = sem("bn_done")
        mv_done = sem("mv_done")
        var_done = sem("var_done")
        rstd_done = sem("rstd_done")
        khi_done = sem("khi_done")
        k_half = sem("k_half")
        k_split = sem("k_split")
        xn_done = sem("xn_done")
        csq_done = sem("csq_done")
        xsq_done = sem("xsq_done")
        xt_done = sem("xt_done")
        ssq_done = sem("ssq_done")
        ssk_done = sem("ssk_done")
        ssq_floor = sem("ssq_floor")
        ssk_floor = sem("ssk_floor")
        rq_done = sem("rq_done")
        rk_done = sem("rk_done")
        wq_done = sem("wq_done")
        rq_ready = sem("rq_ready")
        q_done = sem("q_done")
        qhi_done = sem("qhi_done")
        q_split = sem("q_split")
        q_twice = sem("q_twice")
        v_ready = sem("v_ready")
        v_taken = sem("v_taken")
        scores_ready = sem("scores_ready")
        exp_done = sem("exp_done")
        pv_done = sem("pv_done")
        sum_taken = sem("sum_taken")
        o_taken = [sem(f"o_taken{h}") for h in range(2)]
        inv_done = sem("inv_done")
        on_done = sem("on_done")
        x2_done = sem("x2_done")
        bn2_done = sem("bn2_done")
        mv2_done = sem("mv2_done")
        var2_done = sem("var2_done")
        rstd2_done = sem("rstd2_done")
        x2n_done = sem("x2n_done")
        x2t_ready = sem("x2t_ready")
        x2t_taken = sem("x2t_taken")
        logit_ready = sem("logit_ready")
        logit_done = sem("logit_done")
        x2_stored = sem("x2_stored")
        x2n_stored = [sem(f"x2n_stored{n}") for n in range(2)]
        step = sem("step")
        e_neg = sem("e_neg")
        margin_done = sem("margin_done")
        key_set = sem("key_set")
        key_done = sem("key_done")
        key_t = sem("key_t")
        thr_done = sem("thr_done")
        signs_done = sem("signs_done")
        enough_done = sem("enough_done")
        n_ready = sem("n_ready")
        pick_done = sem("pick_done")
        t_ready = sem("t_ready")
        mask_done = sem("mask_done")
        pre_ready = sem("pre_ready")
        pay_done = sem("pay_done")
        oh_done = sem("oh_done")
        found_ready = sem("found_ready")
        idx_done = sem("idx_done")
        prob_done = sem("prob_done")
        got_clear = sem("got_clear")
        raw_in = [sem(f"raw_in{n}") for n in range(RAW_BUFS)]
        whi_done = sem("whi_done")
        wlo_done = sem("wlo_done")
        z_ready = sem("z_ready")
        gelu_done = sem("gelu_done")
        h_split = sem("h_split")
        x_gathered = [sem(f"x_gathered{t}") for t in range(ST)]
        o_gathered = sem("o_gathered")
        xt_ready = sem("xt_ready")
        xthi_done = sem("xthi_done")
        xt_split = sem("xt_split")
        acc_ready = sem("acc_ready")
        y_done = sem("y_done")
        scattered = sem("scattered")

        block = stack.enter_context(nc.Block())

        def number(u):
            return 2 * u[0] + u[1]

        def after(u):
            return (u[0], 1) if u[1] == 0 else (u[0] + 1, 0)

        def before(u):
            return (u[0], 0) if u[1] == 1 else (u[0] - 1, 1)

        def run_units(engine, unit):
            last = UNITS // 2 - 1
            unit((0, 0), 0, 3)
            unit((0, 1), 1, 3)
            unit((1, 0), 2, 3)
            with engine.Fori(1, last - 1) as h:
                unit((h, 1), 3, 3)
                unit((h + 1, 0), 3, 3)
            unit((last - 1, 1), 3, 2)
            unit((last, 0), 3, 1)
            unit((last, 1), 3, 0)

        def run_experts(engine, expert):
            with engine.Fori(0, E - 1) as e:
                expert(e, False)
            expert(E - 1, True)

        def raw_halves(n):
            return (raw[n][:, 0:HALF].rearrange("p (k c) -> p k c", k=KD),
                    raw[n][:, HALF:2 * HALF].rearrange("p (m d) -> p m d", m=CHUNK_M))

        @block.sync
        def _(sp):
            def load_x(u):
                n = number(u)
                sp.dma_start(x_all[:, bass.ds(n, 1), :],
                             x_rows[bass.ds(n * P, P), :].rearrange("p (a d) -> p a d", a=1)
                             ).then_inc(x_in[u[1]], 16)

            def load_c(u):
                sp.dma_start(c_sb[u[1]][:, :], c_rows[bass.ds(number(u) * P, P), :]).then_inc(c_in[u[1]], 16)

            def load_chunk(e, c):
                n = c % RAW_BUFS
                up, down = raw_halves(n)
                sp.dma_start(up, W1[bass.ds(e, 1), :, c * CW:(c + 1) * CW]
                             .rearrange("a (k p) c -> p (a k) c", p=P)).then_inc(raw_in[n], 16)
                sp.dma_start(down, W2[bass.ds(e, 1), c * CW:(c + 1) * CW, :]
                             .rearrange("a (m p) d -> p (a m) d", p=P)).then_inc(raw_in[n], 16)

            load_x((0, 0))
            load_c((0, 0))
            sp.dma_start(ident, consts[:, C_IDENT:C_IDENT + P]).then_inc(ident_in, 16)
            sp.dma_start(cst[:, C_BEFORE:], consts[:, C_BEFORE:]).then_inc(cst_in, 16)
            sp.dma_start(wg[:, :, :], Wg.rearrange("(k p) e -> p k e", p=P)).then_inc(wg_in, 16)
            load_x((0, 1))
            load_c((0, 1))
            sp.dma_start(bgb[:, :], bg.rearrange("(a e) -> a e", a=1).broadcast_to([P, E])).then_inc(bg_in, 16)

            def store_unit(u):
                n = number(u)
                sp.wait_ge(x2_done, n + 1)
                sp.dma_start(out_rows[bass.ds(n * P, P), :].rearrange("p (a d) -> p a d", a=1),
                             x_all[:, bass.ds(n, 1), :]).then_inc(x2_stored, 16)
                sp.wait_ge(x2n_done, n + 1)
                sp.dma_start(x2n_dram[bass.ds(n * P, P), :], x2n[u[1]][:, :]).then_inc(x2n_stored[u[1]], 16)

            def load_next(u):
                n = number(u)
                sp.wait_ge(xn_done, n - 1)
                load_x(u)
                sp.wait_ge(k_split, n - 1)
                sp.wait_ge(v_ready, n - 1)
                load_c(u)

            load_next((1, 0))
            load_next((1, 1))
            for c in range(RAW_BUFS):
                load_chunk(0, c)
            load_next((2, 0))
            store_unit((0, 0))
            end = UNITS // 2 - 1
            with sp.Fori(2, end) as h:
                load_next((h, 1))
                store_unit((h - 2, 1))
                load_next((h + 1, 0))
                store_unit((h - 1, 0))
            load_next((end, 1))
            for u in ((end - 2, 1), (end - 1, 0), (end - 1, 1), (end, 0), (end, 1)):
                store_unit(u)

            def expert(e, last):
                for c in range(CHUNKS):
                    k = c + RAW_BUFS
                    if last and k >= CHUNKS:
                        break
                    sp.wait_ge(wlo_done, e * CHUNKS + c + 1)
                    load_chunk(e if k < CHUNKS else e + 1, k % CHUNKS)

            run_experts(sp, expert)
            sp.wait_ge(x2_stored, 16 * UNITS)
            for n in range(2):
                sp.wait_ge(x2n_stored[n], 16 * UNITS // 2)
            sp.wait_ge(scattered, 16 * ST * E)

        @block.gpsimd
        def _(pool):
            def inv_sqrt(dst, src, n):
                return nc.gpsimd.tensor_tensor(dst, src, power[:, 0:n], ALU.pow)

            nc.gpsimd.memset(power[:, :], -0.5).then_inc(power_set, 1)
            for n in range(2):
                nc.gpsimd.memset(v_t[n][:, :, 1:3, :], 1.0).then_inc(v_ones, 1)
            pool.wait_ge(power_set, 1)

            def prepare(u):
                pool.wait_ge(var_done, number(u) + 1)
                inv_sqrt(rstd[:, :], var_e[:, :], 1).then_inc(rstd_done, 1)

            def query_norms(u):
                pool.wait_ge(ssq_floor, number(u) + 1)
                inv_sqrt(rnorm[u[1]][:, 1, :, :].rearrange("p t h -> p (t h)"), ss_max[:, 8:16], 8
                         ).then_inc(rq_done, 1)

            def key_norms(u):
                pool.wait_ge(ssk_floor, number(u) + 1)
                inv_sqrt(rnorm[u[1]][:, 0, :, :].rearrange("p t h -> p (t h)"), ss_max[:, 0:8], 8
                         ).then_inc(rk_done, 1)

            def key_remainders(u, prepared):
                n = number(u)
                pool.wait_ge(khi_done, n + 1)
                if prepared:
                    pool.wait_ge(rstd_done, n + 2)
                else:
                    pool.wait_ge(rq_done, n + 1)
                for h in range(2):
                    if h == 1:
                        pool.wait_ge(k_half, n + 1)
                    ch = slice(DH * h, DH * (h + 1))
                    nc.gpsimd.tensor_tensor(k_hl[h][u[1]][DH * (1 - h):DH * (2 - h), :], c_sb[u[1]][ch, :],
                                            k_hl[h][u[1]][ch, :].bitcast(F32), ALU.subtract
                                            ).then_inc(k_split if h else k_half, 1)
                pool.wait_ge(k_split, n + 1)

            def finish(u):
                n = number(u)
                pool.wait_ge(var2_done, n + 1)
                inv_sqrt(rstd2[:, :], var2_e[:, :], 1).then_inc(rstd2_done, 1)

            prepare((0, 0))
            prepare((0, 1))
            query_norms((0, 0))
            key_remainders((0, 0), False)
            key_norms((0, 0))
            query_norms((0, 1))
            prepare((1, 0))

            def unit(u, behind, ahead):
                if ahead:
                    key_remainders(after(u), ahead > 1)
                    if behind:
                        pool.wait_ge(exp_done, TT * number(u))
                    key_norms(after(u))
                if behind:
                    finish(before(u))
                if ahead > 1:
                    query_norms(after(after(u)))
                if ahead > 2:
                    prepare(after(after(after(u))))

            run_units(pool, unit)

            def first_low(c):
                pool.wait_ge(whi_done, c + 1)
                nc.gpsimd.tensor_tensor(w_lo[c][:, :], raw[c][:, :], w_hi[c][:, :].bitcast(F32), ALU.subtract
                                        ).then_inc(wlo_done, 1)

            finish((UNITS // 2 - 1, 1))
            for c in range(AHEAD):
                first_low(c)
            pool.wait_ge(logit_done, UNITS)
            pool.wait_ge(x2_stored, 16 * UNITS)
            for n in range(2):
                pool.wait_ge(x2n_stored[n], 16 * UNITS // 2)
            nc.gpsimd.memset(x_got[:, :, :], 0.0).then_inc(got_clear, 1)
            nc.gpsimd.memset(o_got[:, :, :], 0.0).then_inc(got_clear, 1)
            pool.wait_ge(got_clear, 2)

            def gather_x(e):
                pool.wait_ge(idx_done, e + 1)
                for t in range(ST):
                    nc.gpsimd.indirect_dma_start(
                        x_got[:, t, :], None, x2n_dram,
                        bass.IndirectOffsetOnAxis(idx_all[:, e, t:t + 1], 0),
                        bounds_check=N_TOK - 1, oob_is_err=False).then_inc(x_gathered[t], 16)

            gather_x(0)
            for e in range(E):
                if e + 1 < E:
                    pool.wait_ge(xt_ready, ST * (e + 1))
                    gather_x(e + 1)
                if e > 0:
                    pool.wait_ge(scattered, 16 * ST * e)
                for t in range(ST):
                    nc.gpsimd.indirect_dma_start(
                        o_got[:, t, :], None, out_rows,
                        bass.IndirectOffsetOnAxis(idx_all[:, e, t:t + 1], 0),
                        bounds_check=N_TOK - 1, oob_is_err=False).then_inc(o_gathered, 16)
                for t in range(ST):
                    pool.wait_ge(y_done, ST * (e + 1) + t + 1)
                    nc.gpsimd.indirect_dma_start(
                        out_rows, bass.IndirectOffsetOnAxis(idx_all[:, e, t:t + 1], 0), o_got[:, t, :], None,
                        bounds_check=N_TOK - 1, oob_is_err=False).then_inc(scattered, 16)

        @block.scalar
        def _(act):
            def square_queries(u, reused):
                n = number(u)
                act.wait_ge(xt_done, n + 1)
                if reused:
                    act.wait_ge(ssq_done, n)
                nc.scalar.activation(x_sq[:, :], bank_m[:, :], ACT.Square).then_inc(xsq_done, 1)

            def take_v(u, behind):
                n = number(u)
                act.wait_ge(v_ready, n + 1)
                if behind > 1:
                    act.wait_ge(pv_done, TT * (n - 1))
                nc.scalar.activation(v_t[u[1]][:, :, 0:4:3, :],
                                     bank_t[:, :].rearrange("p (t h d) -> p t h d", t=TT, h=2),
                                     ACT.Copy).then_inc(v_taken, 1)
                if behind:
                    act.wait_ge(ssk_done, n)
                nc.scalar.activation(c_sq[:, :], bank_t[:, :], ACT.Square).then_inc(csq_done, 1)

            def round_keys(u, reused):
                n = number(u)
                act.wait_ge(c_in[u[1]], 16 * (u[0] + 1))
                if reused:
                    act.wait_ge(scores_ready, TT * (n - 1))
                for h in range(2):
                    ch = slice(DH * h, DH * (h + 1))
                    last = nc.scalar.activation(k_hl[h][u[1]][ch, :], c_sb[u[1]][ch, :], ACT.Copy)
                last.then_inc(khi_done, 1)

            def repeat_queries(u):
                act.wait_ge(q_done, number(u) + 1)
                for h in range(2):
                    last = nc.scalar.activation(q_hh[h][u[1]][DH * (1 - h):DH * (2 - h), :],
                                                q_f[DH * h:DH * (h + 1), :], ACT.Copy)
                last.then_inc(q_twice, 1)

            def exponentials(u, t, reused):
                g = TT * number(u) + t
                act.wait_ge(scores_ready, g + 1)
                if reused:
                    act.wait_ge(pv_done, g - 1)
                for h in range(2):
                    last = nc.scalar.activation(prob[h][t % 2][:, :], s_ps[:, 2 * (t % 2) + h, :], ACT.Exp,
                                                scale=rnorm[u[1]][:, 0, t, h:h + 1])
                last.then_inc(exp_done, 1)

            def take_o(u, reused):
                n = number(u)
                act.wait_ge(pv_done, TT * (n + 1))
                if reused:
                    act.wait_ge(on_done, n)
                nc.scalar.activation(p_sum[0:DH, :], o_ps[0][DH:P, :], ACT.Copy)
                nc.scalar.activation(o_sb[0:DH, :], o_ps[0][0:DH, :], ACT.Copy).then_inc(o_taken[0], 1)
                nc.scalar.activation(p_sum[DH:P, :], o_ps[1][0:DH, :], ACT.Copy).then_inc(sum_taken, 1)
                nc.scalar.activation(o_sb[DH:P, :], o_ps[1][DH:P, :], ACT.Copy).then_inc(o_taken[1], 1)

            def take_x2t(u):
                act.wait_ge(x2t_ready, number(u) + 1)
                nc.scalar.activation(x2n_t[:, :, :], bank_t[:, :].rearrange("p (k t) -> p k t", k=KD),
                                     ACT.Copy).then_inc(x2t_taken, 1)

            round_keys((0, 0), False)
            act.wait_ge(v_ones, 2)
            square_queries((0, 0), False)
            take_v((0, 0), 0)
            repeat_queries((0, 0))
            square_queries((0, 1), True)
            act.wait_ge(rk_done, 1)
            exponentials((0, 0), 0, False)

            def unit(u, behind, ahead):
                if ahead:
                    take_v(after(u), behind + 1)
                exponentials(u, 1, behind > 0)
                if ahead:
                    round_keys(after(u), behind > 0)
                if behind > 1:
                    take_x2t(before(before(u)))
                exponentials(u, 2, True)
                if ahead:
                    repeat_queries(after(u))
                exponentials(u, 3, True)
                if ahead > 1:
                    square_queries(after(after(u)), True)
                if ahead:
                    act.wait_ge(rk_done, number(u) + 2)
                    exponentials(after(u), 0, True)
                take_o(u, behind > 0)

            run_units(act, unit)
            take_x2t((UNITS // 2 - 1, 0))

            def split_hi(e, c):
                act.wait_ge(raw_in[c % RAW_BUFS], 32 * ((CHUNKS // RAW_BUFS) * e + c // RAW_BUFS + 1))
                nc.scalar.activation(w_hi[c % SPLIT_BUFS][:, :], raw[c % RAW_BUFS][:, :], ACT.Copy
                                     ).then_inc(whi_done, 1)

            act.wait_ge(key_set, 1)
            nc.scalar.activation(key_w[:, 0:EARLY, :, :], key[:, 0:EARLY, :].unsqueeze(3)
                                 .broadcast_to([P, EARLY, E, WAYS]), ACT.Copy).then_inc(key_done, 1)
            for c in range(AHEAD):
                split_hi(0, c)

            def count_signs(r):
                act.wait_ge(thr_done, r + 1)
                nc.scalar.activation(junk_a[:, :], four_flat[:, 0:SIGNS], ACT.Sign, scale=-1.0, bias=thr[:, 0:1],
                                     accum_out=excess[:, :]).then_inc(signs_done, 1)

            act.wait_ge(key_t, 1)
            count_signs(0)
            take_x2t((UNITS // 2 - 1, 1))
            act.wait_ge(margin_done, 2)
            nc.scalar.activation(p_exp[:, :, :], clamped[:, :, :], ACT.Exp, scale=-1.0).then_inc(e_neg, 1)
            for r in range(1, ROUNDS):
                count_signs(r)
            for t in range(ST):
                act.wait_ge(xt_ready, t + 1)
                nc.scalar.activation(xt_hi[:, 0, :, t * P:(t + 1) * P],
                                     (bank_t, bank_m, *two)[t][:, :].rearrange("p (k t) -> p k t", k=KD),
                                     ACT.Copy).then_inc(xthi_done, 1)

            def expert(e, last):
                for m in range(MT):
                    n = MT * e + m
                    act.wait_ge(z_ready, n + 1)
                    nc.scalar.activation(h_f[m % 2][:, :], z_ps[m % 2][:, :], ACT.Gelu)
                    nc.scalar.activation(h_hi[m % 2][:, :], z_ps[m % 2][:, :], ACT.Gelu).then_inc(gelu_done, 1)
                    if m % CHUNK_M == 0:
                        c = m // CHUNK_M + AHEAD
                        if c < CHUNKS:
                            split_hi(e, c)
                        elif not last:
                            split_hi(e + 1, c - CHUNKS)

            run_experts(act, expert)

        @block.vector
        def _(dve):
            def statistics(u):
                n = number(u)
                dve.wait_ge(x_in[u[1]], 16 * (u[0] + 1))
                nc.vector.bn_stats(stats[:, :], x_all[:, bass.ds(n, 1), :].rearrange("p a d -> p (a d)")
                                   ).then_inc(bn_done, 1)
                dve.wait_ge(bn_done, n + 1)
                nc.vector.memset(pad[:, :], 0.0)
                nc.vector.bn_aggr(mv[:, :], stats[:, :]).then_inc(mv_done, 1)
                dve.wait_ge(mv_done, n + 1)
                nc.vector.tensor_scalar(var_e[:, :], mv[:, 1:2], LN_EPS, None, ALU.add).then_inc(var_done, 1)

            def normalize(u):
                n = number(u)
                dve.wait_ge(rstd_done, n + 1)
                nc.vector.tensor_scalar(x_norm[:, :], x_all[:, bass.ds(n, 1), :].rearrange("p a d -> p (a d)"),
                                        mv[:, 0:1], rstd[:, 0:1], ALU.subtract, ALU.mult).then_inc(xn_done, 1)

            def sum_query_squares(u):
                n = number(u)
                dve.wait_ge(xsq_done, n + 1)
                nc.vector.tensor_reduce(ss[:, 8:16], x_sq[:, :].rearrange("p (g d) -> p g d", d=DH), AX_X,
                                        ALU.add).then_inc(ssq_done, 1)
                dve.wait_ge(ssq_done, n + 1)
                nc.vector.tensor_scalar(ss_max[:, 8:16], ss[:, 8:16], NORM_EPS2, None, ALU.max
                                        ).then_inc(ssq_floor, 1)

            def sum_key_squares(u):
                n = number(u)
                dve.wait_ge(csq_done, n + 1)
                nc.vector.tensor_reduce(ss[:, 0:8], c_sq[:, :].rearrange("p (g d) -> p g d", d=DH), AX_X,
                                        ALU.add).then_inc(ssk_done, 1)
                dve.wait_ge(ssk_done, n + 1)
                nc.vector.tensor_scalar(ss_max[:, 0:8], ss[:, 0:8], NORM_EPS2, None, ALU.max
                                        ).then_inc(ssk_floor, 1)

            def take_logits(u):
                n = number(u)
                dve.wait_ge(logit_ready, n + 1)
                nc.vector.tensor_tensor(logits[:, bass.ds(n, 1), :].rearrange("p a e -> p (a e)"),
                                        bank_t[:, 0:E], bgb[:, :], ALU.add).then_inc(logit_done, 1)

            def queries(u, follow, reused):
                n = number(u)
                dve.wait_ge(rq_ready, n + 1)
                if reused:
                    dve.wait_ge(q_twice, n)
                nc.vector.scalar_tensor_tensor(q_f[:, :], x_norm[:, :], ALPHA, bank_m[:, :], ALU.mult, ALU.mult
                                               ).then_inc(q_done, 1)
                dve.wait_ge(q_done, n + 1)
                for h in range(2):
                    ch = slice(DH * h, DH * (h + 1))
                    last = nc.vector.tensor_copy(q_hh[h][u[1]][ch, :], q_f[ch, :])
                last.then_inc(qhi_done, 1)
                if follow is not None:
                    normalize(follow)
                dve.wait_ge(qhi_done, n + 1)
                for h in range(2):
                    ch = slice(DH * h, DH * (h + 1))
                    last = nc.vector.tensor_tensor(q_lo[u[1]][ch, :], q_f[ch, :],
                                                   q_hh[h][u[1]][ch, :].bitcast(F32), ALU.subtract)
                last.then_inc(q_split, 1)

            def widen_queries(u):
                dve.wait_ge(rq_done, number(u) + 1)
                nc.vector.tensor_copy(wide_q[:, :, :, :], rnorm[u[1]][:, 1, :, :].unsqueeze(3)
                                      .broadcast_to([P, TT, 2, DH])).then_inc(wq_done, 1)

            def invert_sums(u):
                n = number(u)
                dve.wait_ge(sum_taken, n + 1)
                nc.vector.reciprocal(p_inv[:, :], p_sum[:, :]).then_inc(inv_done, 1)

            def residual(u):
                n = number(u)
                xu = x_all[:, bass.ds(n, 1), :].rearrange("p a d -> p (a d)")
                dve.wait_ge(o_taken[1], n + 1)
                dve.wait_ge(inv_done, n + 1)
                nc.vector.tensor_tensor(o_norm[:, :], o_sb[:, :], p_inv[:, :], ALU.mult).then_inc(on_done, 1)
                dve.wait_ge(on_done, n + 1)
                nc.vector.tensor_tensor(xu, xu, o_norm[:, :], ALU.add).then_inc(x2_done, 1)

            def statistics_x2(u):
                n = number(u)
                xu = x_all[:, bass.ds(n, 1), :].rearrange("p a d -> p (a d)")
                dve.wait_ge(x2_done, n + 1)
                nc.vector.memset(pad[:, :], 0.0)
                nc.vector.bn_stats(stats2[:, :], xu).then_inc(bn2_done, 1)
                dve.wait_ge(bn2_done, n + 1)
                nc.vector.memset(pad2[:, :], 0.0)
                nc.vector.bn_aggr(mv2[:, :], stats2[:, :]).then_inc(mv2_done, 1)
                dve.wait_ge(mv2_done, n + 1)
                nc.vector.tensor_scalar(var2_e[:, :], mv2[:, 1:2], LN_EPS, None, ALU.add).then_inc(var2_done, 1)

            def normalize_x2(u, reused):
                n = number(u)
                xu = x_all[:, bass.ds(n, 1), :].rearrange("p a d -> p (a d)")
                dve.wait_ge(rstd2_done, n + 1)
                if reused:
                    dve.wait_ge(x2n_stored[u[1]], 16 * u[0])
                nc.vector.tensor_scalar(x2n[u[1]][:, :], xu, mv2[:, 0:1], rstd2[:, 0:1], ALU.subtract, ALU.mult
                                        ).then_inc(x2n_done, 1)

            statistics((0, 0))
            normalize((0, 0))
            statistics((0, 1))
            sum_query_squares((0, 0))
            widen_queries((0, 0))
            sum_key_squares((0, 0))
            queries((0, 0), None, False)
            normalize((0, 1))
            dve.wait_ge(cst_in, 16)
            dve.wait_ge(bg_in, 16)
            nc.vector.tensor_copy(before_b[:, :], cst[:, C_BEFORE:C_BEFORE + P]).then_inc(bf_done, 1)
            nc.vector.tensor_copy(ones_b[:, :], cst[:, C_ONES:C_ONES + P]).then_inc(bf_done, 1)
            nc.vector.tensor_copy(block_b[:, :], cst[:, C_BLOCK:C_BLOCK + P]).then_inc(bf_done, 1)
            for n in range(2):
                nc.vector.tensor_copy(parts[:, :, :, n], cst[:, C_TOK + n * UNITS:C_TOK + (n + 1) * UNITS]
                                      .unsqueeze(1).broadcast_to([P, E, UNITS])).then_inc(bf_done, 1)
            sum_query_squares((0, 1))
            statistics((1, 0))
            widen_queries((0, 1))

            def unit(u, behind, ahead):
                if behind:
                    invert_sums(before(u))
                if ahead:
                    sum_key_squares(after(u))
                    queries(after(u), after(after(u)) if ahead > 1 else None, True)
                if behind:
                    residual(before(u))
                    statistics_x2(before(u))
                if ahead > 1:
                    sum_query_squares(after(after(u)))
                if behind:
                    normalize_x2(before(u), behind > 2)
                if behind > 1:
                    take_logits(before(before(u)))
                if ahead > 2:
                    statistics(after(after(after(u))))
                if ahead > 1:
                    widen_queries(after(after(u)))

            run_units(dve, unit)
            end = (UNITS // 2 - 1, 1)

            done = [0]

            def put(ins):
                done[0] += 1
                ins.then_inc(step, 1)

            def link(ins):
                put(ins)
                dve.wait_ge(step, done[0])

            def keys_of(a, b):
                four_d = [P, b - a, E, E]
                l_j = logits[:, a:b, :].unsqueeze(2).broadcast_to(four_d)
                l_i = logits[:, a:b, :].unsqueeze(3).broadcast_to(four_d)
                tie = cst[:, C_TIE:C_TIE + E * E].rearrange("p (i j) -> p i j", i=E).unsqueeze(1).broadcast_to(four_d)
                offd = cst[:, C_OFFD:C_OFFD + E * E].rearrange("p (i j) -> p i j", i=E).unsqueeze(1).broadcast_to(four_d)
                put(nc.vector.tensor_tensor(cmp_a[:, a:b, :, :], l_j, l_i, ALU.is_gt))
                link(nc.vector.tensor_tensor(cmp_b[:, a:b, :, :], l_j, l_i, ALU.is_equal))
                link(nc.vector.tensor_tensor(cmp_b[:, a:b, :, :], cmp_b[:, a:b, :, :], tie, ALU.mult))
                link(nc.vector.tensor_tensor(cmp_a[:, a:b, :, :], cmp_a[:, a:b, :, :], cmp_b[:, a:b, :, :], ALU.add))
                link(nc.vector.tensor_reduce(rank[:, a:b, :], cmp_a[:, a:b, :, :], AX_X, ALU.add))
                link(nc.vector.scalar_tensor_tensor(al[:, a:b, :], rank[:, a:b, :], 1.5, logits[:, a:b, :],
                                                    ALU.is_lt, ALU.mult))
                put(nc.vector.tensor_scalar(key_b[:, a:b, :], rank[:, a:b, :], 1.5, KEY_OUT, ALU.is_ge, ALU.mult))
                link(nc.vector.tensor_tensor(cmp_b[:, a:b, :, :], al[:, a:b, :].unsqueeze(2).broadcast_to(four_d),
                                             offd, ALU.mult))
                link(nc.vector.tensor_reduce(other[:, a:b, :], cmp_b[:, a:b, :, :], AX_X, ALU.add))
                link(nc.vector.tensor_tensor(margin[:, a:b, :], logits[:, a:b, :], other[:, a:b, :], ALU.subtract))
                nc.vector.tensor_scalar(clamped[:, a:b, :], margin[:, a:b, :], KEY_MAX, KEY_MIN,
                                        ALU.min, ALU.max).then_inc(margin_done, 1)
                dve.wait_ge(margin_done, 1 if a == 0 else 2)
                link(nc.vector.tensor_scalar(squeezed[:, a:b, :], clamped[:, a:b, :], 1.0 / KEY_SQUEEZE,
                                             KEY_BEND / KEY_SQUEEZE - KEY_BEND, ALU.mult, ALU.add))
                link(nc.vector.tensor_tensor(bent[:, a:b, :], clamped[:, a:b, :], squeezed[:, a:b, :], ALU.max))
                nc.vector.tensor_tensor(key[:, a:b, :], bent[:, a:b, :], key_b[:, a:b, :], ALU.add
                                        ).then_inc(key_set, 1)

            dve.wait_ge(logit_done, EARLY)
            keys_of(0, EARLY)
            width = KEY_RANGE / WAYS
            put(nc.vector.memset(low[:, :], KEY_LO))
            nc.vector.tensor_scalar(thr[:, :], cst[:, C_KVEC:C_KVEC + 1], width, KEY_LO, ALU.mult, ALU.add
                                    ).then_inc(thr_done, 1)
            invert_sums(end)
            take_logits(before(end))
            residual(end)
            statistics_x2(end)
            normalize_x2(end, True)
            early = EARLY * P
            dve.wait_ge(key_t, 1)
            dve.wait_ge(thr_done, 1)
            link(nc.vector.tensor_scalar(junk[:, 0:early - SIGNS], four_flat[:, SIGNS:early], thr[:, 0:1], None,
                                         ALU.is_ge, ALU.add, accum_out=count0[:, :]))
            dve.wait_ge(signs_done, 1)
            put(nc.vector.scalar_tensor_tensor(rest0[:, :], count0[:, :], -2.0, excess[:, :], ALU.mult, ALU.add))
            take_logits(end)
            dve.wait_ge(logit_done, UNITS)
            keys_of(EARLY, UNITS)
            dve.wait_ge(key_set, 2)
            nc.vector.tensor_copy(key_w[:, EARLY:, :, :], key[:, EARLY:, :].unsqueeze(3)
                                  .broadcast_to([P, UNITS - EARLY, E, WAYS])).then_inc(key_done, 1)

            def part(n):
                return parts[:, :, :, n].rearrange("p e t -> p t e")

            for r in range(ROUNDS):
                final = r == ROUNDS - 1
                if r == 0:
                    dve.wait_ge(key_t, 2)
                    link(nc.vector.tensor_scalar(junk[:, early - SIGNS:], four_flat[:, early:], thr[:, 0:1], None,
                                                 ALU.is_ge, ALU.add, accum_out=count[:, :]))
                else:
                    dve.wait_ge(thr_done, r + 1)
                    link(nc.vector.tensor_scalar(junk[:, :], four_flat[:, SIGNS:], thr[:, 0:1], None,
                                                 ALU.is_ge, ALU.add, accum_out=count[:, :]))
                dve.wait_ge(signs_done, r + 1)
                nc.vector.scalar_tensor_tensor(enough[:, :], count[:, :], 2.0, (excess if r else rest0)[:, :],
                                               ALU.mult, ALU.is_ge).then_inc(enough_done, 1)
                if r < ROUNDS - 2:
                    put(nc.vector.tensor_scalar(thr_base[:, :], cst[:, C_KVEC:C_KVEC + 1], width / WAYS,
                                                low[:, 0:1], ALU.mult, ALU.add))
                if r == 0:
                    dve.wait_ge(e_neg, 1)
                    link(nc.vector.tensor_scalar(p_exp[:, :, :], p_exp[:, :, :], 1.0, None, ALU.add))
                elif r == 1:
                    link(nc.vector.reciprocal(p_sel[:, :, :], p_exp[:, :, :]))
                elif r == 2:
                    link(nc.vector.tensor_copy(part(2), p_sel[:, :, :]))
                elif r == 3:
                    link(nc.vector.tensor_tensor(p_rest[:, :, :], p_sel[:, :, :], part(2), ALU.subtract))
                    link(nc.vector.tensor_copy(part(3), p_rest[:, :, :]))
                elif r == 4:
                    put(nc.vector.tensor_tensor(part(4), p_rest[:, :, :], part(3), ALU.subtract))
                dve.wait_ge(step, done[0])
                dve.wait_ge(n_ready, r + 1)
                n_enough = bank_m[:, 0:1]
                if final:
                    put(nc.vector.tensor_scalar(n_next[:, :], n_enough, 1.0, None, ALU.add))
                    link(nc.vector.scalar_tensor_tensor(low_new[:, :], n_enough, width, low[:, :],
                                                        ALU.mult, ALU.add))
                    link(nc.vector.scalar_tensor_tensor(high[:, :], n_next[:, :], width, low[:, :],
                                                        ALU.mult, ALU.add))
                elif r < ROUNDS - 2:
                    nc.vector.scalar_tensor_tensor(thr[:, :], n_enough, width, thr_base[:, :],
                                                   ALU.mult, ALU.add).then_inc(thr_done, 1)
                    link(nc.vector.scalar_tensor_tensor(low[:, :], n_enough, width, low[:, :],
                                                        ALU.mult, ALU.add))
                    width /= WAYS
                else:
                    link(nc.vector.scalar_tensor_tensor(low[:, :], n_enough, width, low[:, :],
                                                        ALU.mult, ALU.add))
                    width /= WAYS
                    nc.vector.tensor_scalar(thr[:, :], cst[:, C_KVEC:C_KVEC + 1], width, low[:, 0:1],
                                            ALU.mult, ALU.add).then_inc(thr_done, 1)
            for n, end_of in enumerate((low_new, high)):
                nc.vector.tensor_scalar(lowpick[:, n, :], cst[:, C_PICK:C_PICK + E], end_of[:, 0:1], None, ALU.mult
                                        ).then_inc(pick_done, 1)
            dve.wait_ge(t_ready, 1)
            put(nc.vector.tensor_copy(t_low[:, :], bank_t[:, 0:E]))
            link(nc.vector.tensor_copy(t_high[:, :], bank_t[:, E:2 * E]))

            three_d = [P, E, UNITS]
            key_e = key[:, :, :].rearrange("p t e -> p e t")
            put(nc.vector.tensor_tensor(ge[:, :, :], key_e, t_low[:, :].unsqueeze(2).broadcast_to(three_d),
                                        ALU.is_ge))
            link(nc.vector.tensor_tensor(mask[:, :, 0, :], key_e, t_high[:, :].unsqueeze(2).broadcast_to(three_d),
                                         ALU.is_gt))
            nc.vector.tensor_tensor(mask[:, :, 1, :], ge[:, :, :], mask[:, :, 0, :], ALU.subtract
                                    ).then_inc(mask_done, 1)
            put(nc.vector.tensor_scalar(s_c[:, :, :], ge[:, :, :], -NO_SLOT, NO_SLOT, ALU.mult, ALU.add))
            dve.wait_ge(pre_ready, 1)
            flat = E * 2 * UNITS
            link(nc.vector.tensor_tensor_scan(scan[:, :], cst[:, C_RESET:C_RESET + flat], two[0][:, flat:2 * flat],
                                              0.0, ALU.mult, ALU.add))
            link(nc.vector.tensor_tensor(pre[:, :, :, :].rearrange("p e g t -> p (e g t)"), two[0][:, 0:flat],
                                         scan[:, :], ALU.add))
            link(nc.vector.tensor_tensor(pre[:, :, :, :], pre[:, :, :, :], mask[:, :, :, :], ALU.mult))
            link(nc.vector.tensor_tensor(slot[:, :, :], pre[:, :, 0, :], s_c[:, :, :], ALU.add))
            link(nc.vector.tensor_tensor(slot[:, :, :], slot[:, :, :], pre[:, :, 1, :], ALU.add))
            link(nc.vector.tensor_scalar(s_hi[:, :, :], slot[:, :, :], float(P), None, ALU.is_ge))
            for s in range(2, ST):
                link(nc.vector.scalar_tensor_tensor(s_hi[:, :, :], slot[:, :, :], float(s * P), s_hi[:, :, :],
                                                    ALU.is_ge, ALU.add))
            link(nc.vector.scalar_tensor_tensor(s_lo[:, :, :], s_hi[:, :, :], -float(P), slot[:, :, :],
                                                ALU.mult, ALU.add))
            dve.wait_ge(x2_stored, 16 * UNITS)
            for n in range(2):
                dve.wait_ge(x2n_stored[n], 16 * UNITS // 2)

            def one_hot(e, a, b):
                shape = [P, b - a, P]
                nc.vector.tensor_tensor(onehot[e % 2][:, a:b, :],
                                        cst[:, C_IOTA:C_IOTA + P].unsqueeze(1).broadcast_to(shape),
                                        s_lo[:, e, a:b].unsqueeze(2).broadcast_to(shape), ALU.is_equal
                                        ).then_inc(oh_done, 1)

            def payload(e):
                shape = [P, UNITS, ST]
                link(nc.vector.tensor_tensor(sel[:, e, :, :], s_hi[:, e, :].unsqueeze(2).broadcast_to(shape),
                                             cst[:, C_IOTA:C_IOTA + ST].unsqueeze(1).broadcast_to(shape),
                                             ALU.is_equal))
                nc.vector.tensor_tensor(pay[:, e, :, :, :], sel[:, e, :, :].unsqueeze(3).broadcast_to(shape + [PAY]),
                                        parts[:, e, :, :].unsqueeze(2).broadcast_to(shape + [PAY]), ALU.mult
                                        ).then_inc(pay_done, 1)

            def slots_of(e):
                got = four[:, e, 0:ST * PAY].rearrange("p (s c) -> p s c", c=PAY)
                dve.wait_ge(found_ready, e + 1)
                link(nc.vector.tensor_reduce(row[:, e, :], got[:, :, 0:2], AX_X, ALU.add))
                nc.vector.tensor_scalar(idx_all[:, e, :], row[:, e, :], NO_TOKEN, None, ALU.add).then_inc(idx_done, 1)
                nc.vector.tensor_reduce(prob_all[:, e, :], got[:, :, 2:PAY], AX_X, ALU.add).then_inc(prob_done, 1)

            payload(0)
            for a in range(0, UNITS, UNITS // QUARTERS):
                one_hot(0, a, a + UNITS // QUARTERS)
            payload(1)
            slots_of(0)
            one_hot(1, 0, UNITS)
            payload(2)
            payload(3)
            slots_of(1)
            one_hot(2, 0, UNITS)

            def split_lo(e, c):
                n = CHUNKS * e + c
                dve.wait_ge(whi_done, n + 1)
                nc.vector.tensor_tensor(w_lo[c % SPLIT_BUFS][:, :], raw[c % RAW_BUFS][:, :],
                                        w_hi[c % SPLIT_BUFS][:, :].bitcast(F32), ALU.subtract
                                        ).then_inc(wlo_done, 1)

            def split_tokens(e, t, parity):
                g = ST * e + t
                bank = (bank_t, bank_m)[t % 2][:, :].rearrange("p (a k t) -> p a k t", a=1, k=KD)
                hi = xt_hi[:, bass.ds(parity, 1), :, t * P:(t + 1) * P]
                lo = xt_lo[:, bass.ds(parity, 1), :, t * P:(t + 1) * P]
                dve.wait_ge(xt_ready, g + 1)
                nc.vector.tensor_copy(hi, bank).then_inc(xthi_done, 1)
                dve.wait_ge(xthi_done, g + 1)
                nc.vector.tensor_tensor(lo, bank, hi.bitcast(F32), ALU.subtract).then_inc(xt_split, 1)

            for t in range(ST):
                dve.wait_ge(xthi_done, t + 1)
                nc.vector.tensor_tensor(xt_lo[:, 0, :, t * P:(t + 1) * P],
                                        (bank_t, bank_m, *two)[t][:, :].rearrange("p (k t) -> p k t", k=KD),
                                        xt_hi[:, 0, :, t * P:(t + 1) * P].bitcast(F32), ALU.subtract
                                        ).then_inc(xt_split, 1)
            one_hot(3, 0, UNITS)
            slots_of(2)
            slots_of(3)
            dve.wait_ge(prob_done, E)
            nc.vector.memset(credit[:, :], 0.0).then_inc(y_done, ST)

            def expert(e, last):
                for m in range(MT):
                    dve.wait_ge(gelu_done, MT * e + m + 1)
                    nc.vector.tensor_tensor(h_lo[m % 2][:, :], h_f[m % 2][:, :], h_hi[m % 2][:, :].bitcast(F32),
                                            ALU.subtract).then_inc(h_split, 1)
                    if m % CHUNK_M == 0:
                        c = m // CHUNK_M + AHEAD
                        if c < CHUNKS:
                            split_lo(e, c)
                        elif not last:
                            split_lo(e + 1, c - CHUNKS)
                    if not last and XT_AT <= m < XT_AT + ST:
                        split_tokens(e + 1, m - XT_AT, (e + 1) % 2)
                dve.wait_ge(o_gathered, 16 * ST * (e + 1))
                for t in range(ST):
                    dve.wait_ge(acc_ready, ST * e + t + 1)
                    nc.vector.scalar_tensor_tensor(o_got[:, t, :], acc_ps[:, t, :], prob_all[:, bass.ds(e, 1), t],
                                                   o_got[:, t, :], ALU.mult, ALU.add).then_inc(y_done, 1)

            run_experts(dve, expert)

        @block.tensor
        def _(pe):
            def transpose_queries(u):
                pe.wait_ge(xn_done, number(u) + 1)
                for t in range(TT):
                    last = nc.tensor.transpose(bank_m[:, t * P:(t + 1) * P], x_norm[:, t * P:(t + 1) * P], ident)
                last.then_inc(xt_done, 1)

            def values(u):
                pe.wait_ge(c_in[u[1]], 16 * (u[0] + 1))
                for t in range(TT):
                    last = nc.tensor.transpose(bank_t[:, t * P:(t + 1) * P], c_sb[u[1]][:, t * P:(t + 1) * P],
                                               ident)
                last.then_inc(v_ready, 1)

            def spread_queries(u):
                pe.wait_ge(wq_done, number(u) + 1)
                for t in range(TT):
                    last = nc.tensor.transpose(bank_m[:, t * P:(t + 1) * P],
                                               wide_q[:, t, :, :].rearrange("p h d -> p (h d)"), ident)
                last.then_inc(rq_ready, 1)

            def scores(u, t, reused):
                if reused:
                    pe.wait_ge(exp_done, TT * number(u) + t - 1)
                for h in range(2):
                    ch = slice(DH * h, DH * (h + 1))
                    keys = slice(t * P, (t + 1) * P)
                    bank = s_ps[:, 2 * (t % 2) + h, :]
                    nc.tensor.matmul(bank, k_hl[h][u[1]][:, keys], q_hh[h][u[1]][:, :], start=True, stop=False)
                    last = nc.tensor.matmul(bank, k_hl[h][u[1]][ch, keys], q_lo[u[1]][ch, :], start=False, stop=True)
                last.then_inc(scores_ready, 1)

            def weighted_values(u, t, reused=False):
                pe.wait_ge(exp_done, TT * number(u) + t + 1)
                for h in range(2):
                    if reused:
                        pe.wait_ge(o_taken[h], number(u))
                    last = nc.tensor.matmul(o_ps[h][:, :], v_t[u[1]][:, t, 2 * h:2 * h + 2, :]
                                            .rearrange("p a d -> p (a d)"), prob[h][t % 2][:, :],
                                            start=(t == 0), stop=(t == TT - 1))
                last.then_inc(pv_done, 1)

            def transpose_x2(u):
                pe.wait_ge(x2n_done, number(u) + 1)
                for k in range(KD):
                    last = nc.tensor.transpose(bank_t[:, k * P:(k + 1) * P], x2n[u[1]][:, k * P:(k + 1) * P],
                                               ident)
                last.then_inc(x2t_ready, 1)

            def router_logits(u):
                pe.wait_ge(x2t_taken, number(u) + 1)
                for k in range(KD):
                    last = nc.tensor.matmul(bank_t[:, 0:E], x2n_t[:, k, :], wg[:, k, :],
                                            start=(k == 0), stop=(k == KD - 1))
                last.then_inc(logit_ready, 1)

            pe.wait_ge(ident_in, 16)
            transpose_queries((0, 0))
            values((0, 0))
            spread_queries((0, 0))
            pe.wait_ge(q_done, 1)
            transpose_queries((0, 1))
            pe.wait_ge(q_split, 1)
            pe.wait_ge(q_twice, 1)
            pe.wait_ge(k_split, 1)
            scores((0, 0), 0, False)

            def unit(u, behind, ahead):
                n = number(u)
                if behind == 2:
                    pe.wait_ge(wg_in, 16)
                    pe.wait_ge(bf_done, 5)
                scores(u, 1, behind > 0)
                if ahead:
                    if behind > 2:
                        pe.wait_ge(logit_done, n - 2)
                    else:
                        pe.wait_ge(csq_done, n + 1)
                    values(after(u))
                    spread_queries(after(u))
                pe.wait_ge(v_taken, n + 1)
                weighted_values(u, 0, behind > 0)
                scores(u, 2, True)
                if behind > 1:
                    if ahead:
                        pe.wait_ge(csq_done, n + 2)
                    else:
                        pe.wait_ge(logit_done, n - 2)
                    transpose_x2(before(before(u)))
                weighted_values(u, 1)
                scores(u, 3, True)
                if behind > 1:
                    router_logits(before(before(u)))
                if ahead > 1:
                    pe.wait_ge(q_done, n + 2)
                    transpose_queries(after(after(u)))
                weighted_values(u, 2)
                if ahead:
                    pe.wait_ge(q_split, n + 2)
                    pe.wait_ge(q_twice, n + 2)
                    pe.wait_ge(k_split, n + 2)
                    scores(after(u), 0, True)
                weighted_values(u, 3)

            run_units(pe, unit)
            end = (UNITS // 2 - 1, 1)

            def transpose_keys(a, b, part):
                pe.wait_ge(key_done, part)
                for t in range(a, b):
                    last = nc.tensor.transpose(four[:, t // 4, (t % 4) * P:(t % 4 + 1) * P],
                                               key_w[:, t, :, :].rearrange("p e w -> p (e w)"), ident)
                last.then_inc(key_t, 1)

            pe.wait_ge(logit_done, UNITS - 2)
            transpose_x2(before(end))
            router_logits(before(end))
            pe.wait_ge(exp_done, TT * UNITS)
            transpose_keys(0, EARLY, 1)
            pe.wait_ge(logit_done, UNITS - 1)
            transpose_x2(end)
            router_logits(end)
            transpose_keys(EARLY, UNITS, 2)
            for r in range(ROUNDS):
                pe.wait_ge(enough_done, r + 1)
                nc.tensor.matmul(bank_m[:, 0:1], block_b[:, :], enough[:, :], start=True, stop=True
                                 ).then_inc(n_ready, 1)
            pe.wait_ge(pick_done, 2)
            nc.tensor.matmul(bank_t[:, 0:2 * E], cst[:, C_ONES:C_ONES + P],
                             lowpick[:, :, :].rearrange("p n e -> p (n e)"), start=True, stop=True
                             ).then_inc(t_ready, 1)
            pe.wait_ge(mask_done, 1)
            flat = E * 2 * UNITS
            mask_flat = mask[:, :, :, :].rearrange("p e g t -> p (e g t)")
            nc.tensor.matmul(two[0][:, flat:2 * flat], ones_b[:, :], mask_flat, start=True, stop=True)
            nc.tensor.matmul(two[0][:, 0:flat], before_b[:, :], mask_flat, start=True, stop=True
                             ).then_inc(pre_ready, 1)

            def find(e):
                pe.wait_ge(pay_done, e + 1)
                for t in range(UNITS):
                    if e == 0 and t % (UNITS // QUARTERS) == 0:
                        pe.wait_ge(oh_done, t // (UNITS // QUARTERS) + 1)
                    elif t == 0:
                        pe.wait_ge(oh_done, QUARTERS + e)
                    last = nc.tensor.matmul(four[:, e, 0:ST * PAY], onehot[e % 2][:, t, :],
                                            pay[:, e, t, :, :].rearrange("p s c -> p (s c)"),
                                            start=(t == 0), stop=(t == UNITS - 1))
                last.then_inc(found_ready, 1)

            def transpose_tokens(t, bank):
                for k in range(KD):
                    last = nc.tensor.transpose(bank[:, k * P:(k + 1) * P], x_got[:, t, k * P:(k + 1) * P], ident)
                last.then_inc(xt_ready, 1)

            def up(e, m, parity, first=False):
                pe.wait_ge(wlo_done, CHUNKS * e + m // CHUNK_M + 1)
                c, z = (m // CHUNK_M) % SPLIT_BUFS, z_ps[m % 2]

                def term(w_part, x_part, k, start=False, stop=False):
                    w = slice(k * CW + (m % CHUNK_M) * P, k * CW + (m % CHUNK_M + 1) * P)
                    x_k = x_part[:, bass.ds(parity, 1), k, :].rearrange("p a t -> p (a t)")
                    return nc.tensor.matmul(z[:, :], w_part[c][:, w], x_k, start=start, stop=stop)

                if first:
                    for k in range(KD):
                        term(w_hi, xt_hi, k, start=(k == 0))
                        term(w_lo, xt_hi, k)
                    pe.wait_ge(xt_split, ST)
                    for k in range(KD):
                        last = term(w_hi, xt_lo, k, stop=(k == KD - 1))
                else:
                    for k in range(KD):
                        term(w_hi, xt_hi, k, start=(k == 0))
                        term(w_hi, xt_lo, k)
                        last = term(w_lo, xt_hi, k, stop=(k == KD - 1))
                last.then_inc(z_ready, 1)

            def down(e, m):
                c = (m // CHUNK_M) % SPLIT_BUFS
                w = slice(HALF + (m % CHUNK_M) * D, HALF + (m % CHUNK_M + 1) * D)
                pe.wait_ge(h_split, MT * e + m + 1)
                for t in range(ST):
                    if m == 0:
                        pe.wait_ge(y_done, ST * e + t + 1)
                    h = slice(t * P, (t + 1) * P)
                    nc.tensor.matmul(acc_ps[:, t, :], h_hi[m % 2][:, h], w_hi[c][:, w],
                                     start=(m == 0), stop=False)
                    nc.tensor.matmul(acc_ps[:, t, :], h_hi[m % 2][:, h], w_lo[c][:, w], start=False, stop=False)
                    last = nc.tensor.matmul(acc_ps[:, t, :], h_lo[m % 2][:, h], w_hi[c][:, w], start=False,
                                            stop=(m == MT - 1))
                    if m == MT - 1:
                        last.then_inc(acc_ready, 1)

            find(0)
            find(1)
            for t in range(ST):
                pe.wait_ge(x_gathered[t], 16)
                transpose_tokens(t, (bank_t, bank_m, *two)[t])
            find(2)
            pe.wait_ge(xthi_done, ST)
            pe.wait_ge(xt_split, ST - 1)
            up(0, 0, 0, first=True)
            find(3)

            def expert(e, last):
                for m in range(MT):
                    if m < MT - 1:
                        up(e, m + 1, e % 2)
                    elif not last:
                        pe.wait_ge(xt_split, ST * (e + 2))
                        up(e + 1, 0, (e + 1) % 2)
                    down(e, m)
                    if not last and XT_AT <= m < XT_AT + ST:
                        pe.wait_ge(x_gathered[m - XT_AT], 16 * (e + 2))
                        pe.wait_ge(xt_split, ST * (e + 1) + m - XT_AT - 1)
                        transpose_tokens(m - XT_AT, (bank_t, bank_m)[m % 2])

            run_experts(pe, expert)


_INS = ["x", "ctx_2048", "L0_ffn_Wg", "L0_ffn_bg", "L0_ffn_W1", "L0_ffn_W2"]


def kernel(**inputs):
    import concourse.bacc as bacc
    import numpy as np
    from concourse.bass_utils import run_bass_kernel_spmd

    nc = bacc.Bacc("TRN2", target_bir_lowering=False, num_devices=1)
    arrays, args = {}, []
    for name, a in [(n, np.ascontiguousarray(inputs[n])) for n in _INS] + [("consts", constants())]:
        arrays[f"in_{name}"] = a
        args.append(nc.dram_tensor(f"in_{name}", a.shape, F32, kind="ExternalInput").ap())
    out = nc.dram_tensor("out_0", (B, S, D), F32, kind="ExternalOutput").ap()
    xattn_moe_kernel(nc, *args, out)
    r = run_bass_kernel_spmd(nc, [arrays], core_ids=[0])
    return r.results[0]["out_0"]
```
